# Optimizing a Trainium2 kernel written in Bass

```python
import numpy as np
import jax
import jax.numpy as jnp

def _softmax(x, axis=-1):
    return jax.nn.softmax(x, axis=axis)

def _gelu(x):
    return jax.nn.gelu(x, approximate=True)

def _silu(x):
    return jax.nn.silu(x)

def _sigmoid(x):
    return jax.nn.sigmoid(x)

def _layernorm(x, axis=-1, eps=1e-05):
    m = jnp.mean(x, axis=axis, keepdims=True)
    v = jnp.var(x, axis=axis, keepdims=True)
    return (x - m) / jnp.sqrt(v + eps)

def _scatter_add(tgt, idx, src, axis=0):
    return tgt.at[idx].add(src)

def _segment_sum(src, seg, n):
    return jax.ops.segment_sum(src, seg, n)
kernel_name = 'mk_gnn_ffn_d1_gnn_r8_9b30be'

def setup_inputs(seed: int=0):
    np.random.seed(seed)
    _w = jnp.asarray

    def _rec_inputs():
        import jax
        import jax.numpy as jnp
        _gk = jax.random.key(seed)
        x = -6.415e-05 + 1 * jax.random.normal(jax.random.fold_in(_gk, 1), (1250, 512), jnp.float32)
        _s = jax.random.randint(jax.random.fold_in(_gk, 2), (10000,), 0, 1250, jnp.int32)
        _d = jax.random.randint(jax.random.fold_in(_gk, 3), (10000,), 0, 1250, jnp.int32)
        _loop = jnp.arange(1250, dtype=jnp.int32)
        src = jnp.concatenate([_s, _d, _loop])
        dst = jnp.concatenate([_d, _s, _loop])
        _o = jnp.argsort(dst, stable=True)
        src = src[_o]
        dst = dst[_o]
        edge_attr_64 = 0.000279952 + 1.00013 * jax.random.normal(jax.random.fold_in(_gk, 11), (21250, 64), jnp.float32)
        return (x, src, dst, edge_attr_64)
    x, src, dst, edge_attr_64 = _rec_inputs()

    def _L0_gnn_setup():
        import jax, jax.numpy as jnp
        import numpy as np
        N_NODES = 2500
        N_EDGES = 40000
        HIDDEN = 512
        EDGE_DIM = 64
        LN_EPS = 1e-05

        def mish(x):
            return x * jnp.tanh(jax.nn.softplus(x))
        key = jax.random.key(seed)
        ks = jax.random.split(key, 8)
        s = lambda fan_in: 1.0 / np.sqrt(fan_in)
        return {'x': jax.random.normal(ks[0], (N_NODES, HIDDEN), dtype=jnp.float32), 'edge_index': jax.random.randint(ks[1], (2, N_EDGES), 0, N_NODES, dtype=jnp.int64), 'edge_attr': jax.random.normal(ks[2], (N_EDGES, EDGE_DIM), dtype=jnp.float32), 'W1': jax.random.normal(ks[3], (2 * HIDDEN + EDGE_DIM, HIDDEN), dtype=jnp.float32) * s(2 * HIDDEN + EDGE_DIM), 'b1': jnp.zeros((HIDDEN,), dtype=jnp.float32), 'W2': jax.random.normal(ks[4], (HIDDEN, HIDDEN), dtype=jnp.float32) * s(HIDDEN), 'b2': jnp.zeros((HIDDEN,), dtype=jnp.float32), 'W3': jax.random.normal(ks[5], (2 * HIDDEN, HIDDEN), dtype=jnp.float32) * s(2 * HIDDEN), 'b3': jnp.zeros((HIDDEN,), dtype=jnp.float32), 'W4': jax.random.normal(ks[6], (HIDDEN, HIDDEN), dtype=jnp.float32) * s(HIDDEN), 'b4': jnp.zeros((HIDDEN,), dtype=jnp.float32), 'gamma': jnp.ones((HIDDEN,), dtype=jnp.float32), 'beta': jnp.zeros((HIDDEN,), dtype=jnp.float32)}
    _L0_gnn_all = _L0_gnn_setup()
    _L0_gnn_in = {k: v for k, v in _L0_gnn_all.items() if k in ('W1', 'b1', 'W2', 'b2', 'W3', 'b3', 'W4', 'b4', 'gamma', 'beta')}
    del _L0_gnn_all

    def _L0_ffn_setup():
        import jax, jax.numpy as jnp
        import numpy as np
        from jax import lax
        N_HEADS = 8
        D_KEYS = 128
        HALF = D_KEYS // 2
        N_KEYS = 256
        TOP_K = 8
        D_MODEL = 512

        def _forward(queries, Wq, bq, keys, w_down, w_up):
            N, T, D = queries.shape
            x = queries.reshape(-1, D)
            q = (x @ Wq + bq).reshape(-1, N_HEADS, D_KEYS)
            q1, q2 = (q[..., :HALF], q[..., HALF:])
            s1 = jnp.einsum('bhc,hnc->bhn', q1, keys[:, 0])
            s2 = jnp.einsum('bhc,hnc->bhn', q2, keys[:, 1])
            s1t, i1 = lax.top_k(s1, TOP_K)
            s2t, i2 = lax.top_k(s2, TOP_K)
            all_scores = (s1t[..., :, None] + s2t[..., None, :]).reshape(-1, N_HEADS, TOP_K * TOP_K)
            all_idx = (i1[..., :, None] * N_KEYS + i2[..., None, :]).reshape(-1, N_HEADS, TOP_K * TOP_K)
            scores, best = lax.top_k(all_scores, TOP_K)
            indices = jnp.take_along_axis(all_idx, best, axis=-1)
            w_d = w_down[indices]
            w_u = w_up[indices]
            inner = jnp.einsum('bd,bhkd->bhk', x, w_d)
            vals = jax.nn.relu(inner) * jax.nn.softmax(scores, axis=-1)
            out = jnp.einsum('bhk,bhkd->bd', vals, w_u)
            return out.reshape(N, T, D)
        key = jax.random.key(seed)
        ks = jax.random.split(key, 6)
        N, T = (2, 1024)
        queries = jax.random.normal(ks[0], (N, T, D_MODEL), dtype=jnp.float32)
        Wq = jax.random.normal(ks[1], (D_MODEL, N_HEADS * D_KEYS), dtype=jnp.float32) / np.sqrt(D_MODEL)
        bq = jnp.zeros((N_HEADS * D_KEYS,), dtype=jnp.float32)
        bound = 1.0 / np.sqrt(HALF)
        keys = jax.random.uniform(ks[2], (N_HEADS, 2, N_KEYS, HALF), dtype=jnp.float32, minval=-bound, maxval=bound)
        w_down = jax.random.normal(ks[3], (N_KEYS * N_KEYS, D_MODEL), dtype=jnp.float32) * 0.02
        w_up = jax.random.normal(ks[4], (N_KEYS * N_KEYS, D_MODEL), dtype=jnp.float32) * 0.02
        return {'queries': queries, 'Wq': Wq, 'bq': bq, 'keys': keys, 'w_down': w_down, 'w_up': w_up}
    _L0_ffn_all = _L0_ffn_setup()
    _L0_ffn_in = {k: v for k, v in _L0_ffn_all.items() if k in ('Wq', 'bq', 'keys', 'w_down', 'w_up')}
    del _L0_ffn_all
    return {'x': x, 'src': src, 'dst': dst, 'edge_attr_64': edge_attr_64, 'L0_gnn_W1': _L0_gnn_in['W1'], 'L0_gnn_b1': _L0_gnn_in['b1'], 'L0_gnn_W2': _L0_gnn_in['W2'], 'L0_gnn_b2': _L0_gnn_in['b2'], 'L0_gnn_W3': _L0_gnn_in['W3'], 'L0_gnn_b3': _L0_gnn_in['b3'], 'L0_gnn_W4': _L0_gnn_in['W4'], 'L0_gnn_b4': _L0_gnn_in['b4'], 'L0_gnn_gamma': _L0_gnn_in['gamma'], 'L0_gnn_beta': _L0_gnn_in['beta'], 'L0_ffn_Wq': _L0_ffn_in['Wq'], 'L0_ffn_bq': _L0_ffn_in['bq'], 'L0_ffn_keys': _L0_ffn_in['keys'], 'L0_ffn_w_down': _L0_ffn_in['w_down'], 'L0_ffn_w_up': _L0_ffn_in['w_up']}

def reference(x, src, dst, edge_attr_64, L0_gnn_W1, L0_gnn_b1, L0_gnn_W2, L0_gnn_b2, L0_gnn_W3, L0_gnn_b3, L0_gnn_W4, L0_gnn_b4, L0_gnn_gamma, L0_gnn_beta, L0_ffn_Wq, L0_ffn_bq, L0_ffn_keys, L0_ffn_w_down, L0_ffn_w_up):
    import jax
    import jax.numpy as jnp

    def _L0_gnn_ref(x, edge_index, edge_attr, W1, b1, W2, b2, W3, b3, W4, b4, gamma, beta):
        import jax, jax.numpy as jnp
        import numpy as np
        N_NODES = 2500
        N_EDGES = 40000
        HIDDEN = 512
        EDGE_DIM = 64
        LN_EPS = 1e-05

        def mish(x):
            return x * jnp.tanh(jax.nn.softplus(x))
        src, dst = (edge_index[0], edge_index[1])
        edge_feat = jnp.concatenate([x[src], x[dst], edge_attr], axis=-1)
        h = mish(edge_feat @ W1 + b1)
        messages = mish(h @ W2 + b2)
        agg = jax.ops.segment_sum(messages, dst, num_segments=x.shape[0])
        u = mish(jnp.concatenate([x, agg], axis=-1) @ W3 + b3)
        out = u @ W4 + b4
        y = x + out
        mu = jnp.mean(y, axis=-1, keepdims=True)
        var = jnp.mean(jnp.square(y - mu), axis=-1, keepdims=True)
        return (y - mu) * jax.lax.rsqrt(var + LN_EPS) * gamma + beta

    def _L0_ffn_ref(queries, Wq, bq, keys, w_down, w_up):
        import jax, jax.numpy as jnp
        import numpy as np
        from jax import lax
        N_HEADS = 8
        D_KEYS = 128
        HALF = D_KEYS // 2
        N_KEYS = 256
        TOP_K = 8
        D_MODEL = 512

        def _forward(queries, Wq, bq, keys, w_down, w_up):
            N, T, D = queries.shape
            x = queries.reshape(-1, D)
            q = (x @ Wq + bq).reshape(-1, N_HEADS, D_KEYS)
            q1, q2 = (q[..., :HALF], q[..., HALF:])
            s1 = jnp.einsum('bhc,hnc->bhn', q1, keys[:, 0])
            s2 = jnp.einsum('bhc,hnc->bhn', q2, keys[:, 1])
            s1t, i1 = lax.top_k(s1, TOP_K)
            s2t, i2 = lax.top_k(s2, TOP_K)
            all_scores = (s1t[..., :, None] + s2t[..., None, :]).reshape(-1, N_HEADS, TOP_K * TOP_K)
            all_idx = (i1[..., :, None] * N_KEYS + i2[..., None, :]).reshape(-1, N_HEADS, TOP_K * TOP_K)
            scores, best = lax.top_k(all_scores, TOP_K)
            indices = jnp.take_along_axis(all_idx, best, axis=-1)
            w_d = w_down[indices]
            w_u = w_up[indices]
            inner = jnp.einsum('bd,bhkd->bhk', x, w_d)
            vals = jax.nn.relu(inner) * jax.nn.softmax(scores, axis=-1)
            out = jnp.einsum('bhk,bhkd->bd', vals, w_u)
            return out.reshape(N, T, D)
        return _forward(queries, Wq, bq, keys, w_down, w_up)
    edge_index = jnp.stack([src, dst])
    x = x + _L0_gnn_ref(_layernorm(x, axis=-1), edge_index, edge_attr_64, L0_gnn_W1, L0_gnn_b1, L0_gnn_W2, L0_gnn_b2, L0_gnn_W3, L0_gnn_b3, L0_gnn_W4, L0_gnn_b4, L0_gnn_gamma, L0_gnn_beta)
    x = x + _L0_ffn_ref(_layernorm(x, axis=-1)[None], L0_ffn_Wq, L0_ffn_bq, L0_ffn_keys, L0_ffn_w_down, L0_ffn_w_up)[0]
    return x

_drawn_inputs = setup_inputs


def setup_inputs(seed=0):
    import zlib

    import numpy as np

    out = dict(_drawn_inputs(seed))
    spreads = {'L0_gnn_b1': (0.0, 0.1),
     'L0_gnn_b2': (0.0, 0.1),
     'L0_gnn_b3': (0.0, 0.494),
     'L0_gnn_b4': (0.0, 0.377),
     'L0_gnn_gamma': (1.0, 0.2),
     'L0_gnn_beta': (0.0, 0.1),
     'L0_ffn_bq': (0.0, 0.8)}
    factors = {'L0_ffn_Wq': 8.0, 'L0_ffn_keys': 8.0, 'L0_ffn_w_down': 8.0, 'L0_ffn_w_up': 8.0}
    for name, (base, spread) in spreads.items():
        noise = np.random.default_rng([zlib.crc32(name.encode()), seed]).standard_normal(out[name].shape)
        drawn = base * np.exp(spread * noise) if base else spread * noise
        out[name] = jnp.asarray(drawn.astype(out[name].dtype))
    for name, factor in factors.items():
        out[name] = (out[name] * factor).astype(out[name].dtype)
    return out
```

```python
import concourse.bass as bass
from concourse import mybir
from contextlib import ExitStack


def gnn_peer_kernel(nc, x, src_cols, dst_cols, dst_row, ea_t, W1, b1, W2, b2, W3, b3, W4, b4,
                    gamma, beta, Wq, bq_cols, keys_t, w_du, out):
    f32, bf16 = mybir.dt.float32, mybir.dt.bfloat16
    i32, u32 = mybir.dt.int32, mybir.dt.uint32
    ALU = mybir.AluOpType
    ACT = mybir.ActivationFunctionType
    AX = mybir.AxisListType.X

    NODES, D = x.shape
    EC, EDGES = ea_t.shape
    R = src_cols.shape[0]
    NT = NODES // R
    ET = EDGES // R
    KC = D // 128
    HEADS, TOPK = 8, 8
    HALF = keys_t.shape[0] // 2
    NKEYS = keys_t.shape[1] // HEADS
    PICKS = HEADS * TOPK
    CPT = ET // NT
    EPS = 1e-5
    LN2 = 0.6931471805599453
    ACT_TABLES = "natural_log_exp_and_others"
    UMAX = 1e9
    RING = 16
    assert NT * R == NODES and ET * R == EDGES and CPT * NT == ET and NT % 2 == 0

    ctx = ExitStack()
    with ctx:
        def sb(name, shape, dt=f32):
            return ctx.enter_context(nc.sbuf_tensor(name, shape, dt))

        def sem(name):
            return ctx.enter_context(nc.semaphore(name))

        def sems(name, n):
            return [sem(f"{name}{k}") for k in range(n)]

        def static(i):
            return isinstance(i, int)

        def need(eng, s, value):
            if not isinstance(value, int) or value > 0:
                eng.wait_ge(s, value)

        def wait_alone(eng, s, value):
            need(eng, s, value)
            if not isinstance(value, int):
                eng.sem_inc(passed, 1)

        P_d = nc.dram_tensor("P_d", (NODES, D), f32, kind="Internal").ap()
        Q_d = nc.dram_tensor("Q_d", (NODES, D), f32, kind="Internal").ap()
        R_d = nc.dram_tensor("R_d", (NODES, D), f32, kind="Internal").ap()
        xn_d = nc.dram_tensor("xn_d", (NODES, D), f32, kind="Internal").ap()
        x2_d = nc.dram_tensor("x2_d", (NODES, D), f32, kind="Internal").ap()
        xf_d = nc.dram_tensor("xf_d", (NODES, D), f32, kind="Internal").ap()
        agg_d = [nc.dram_tensor(f"agg{k}_d", (NODES + R, D), f32, kind="Internal").ap() for k in range(2)]

        ident = sb("ident", [128, 128])
        before = sb("before", [128, 128])
        srcc = sb("srcc", [R, ET], i32)
        dsti = sb("dsti", [R, ET], i32)
        dstf = sb("dstf", [R, ET])
        sidx = sb("sidx", [R, ET], i32)
        dummy = sb("dummy_row", [R, 1])
        ones = sb("ones", [R, 128])
        cnt = sb("cnt", [R, ET])
        cnts = sb("cnts", [R, 1])
        shared = sb("shared", [1, 1], i32)
        eps = sb("eps", [128, 1])
        ln2 = sb("ln2", [128, 1])
        b1b, b2b, b3b, b4b = (sb(n, [128, D]) for n in ("b1b", "b2b", "b3b", "b4b"))
        gab, beb = sb("gab", [128, D]), sb("beb", [128, D])
        bqc = sb("bqc", [128, HEADS])
        iota8 = sb("iota8", [R, TOPK])
        w1a = sb("w1a", [128, 2 * KC, D])
        w1c = sb("w1c", [EC, D])
        w2 = sb("w2", [128, KC, D])
        w3x = sb("w3x", [128, KC, D])
        wide = sb("wide", [128, 20480])
        wq = sb("wq", [128, KC, HEADS * 128])
        keys = sb("keys", [128, HEADS * NKEYS])
        banks = [ctx.enter_context(nc.psum_tensor(f"bank{k}", [128, 512], f32)) for k in range(8)]
        w3a, w4 = w1a[:, 0:KC, :], w1a[:, KC:2 * KC, :]

        def carve(at, rows, *dims):
            n = 1
            for d in dims:
                n *= d
            v = wide[0:rows, at:at + n]
            if len(dims) == 2:
                v = v.rearrange("p (a b) -> p a b", a=dims[0])
            elif len(dims) == 3:
                v = v.rearrange("p (a b c) -> p a b c", a=dims[0], b=dims[1])
            return v, at + n

        c_in, c_w1, c_w3, c_cst, c_cst2 = sem("c_in"), sem("c_w1"), sem("c_w3"), sem("c_cst"), sem("c_cst2")
        passed = sem("passed")
        c_idx, c_wlate = sem("c_idx"), sem("c_wlate")
        n_x, n_row = sems("n_x", 2), sems("n_row", 2)
        n_stat, n_mv, n_lv, n_rs, n_xn = (sem(n) for n in ("n_stat", "n_mv", "n_lv", "n_rs", "n_xn"))
        n_T, n_xt, n_mm, n_ev, n_evp = (sem(n) for n in ("n_T", "n_xt", "n_mm", "n_ev", "n_evp"))
        n_dc, n_dup, n_dd, n_m, n_sx = (sem(n) for n in ("n_dc", "n_dup", "n_dd", "n_m", "n_sx"))
        n_cs, n_any, n_sh = sem("n_cs"), sem("n_any"), sem("n_sh")
        n_st, n_sto, n_zero = sems("n_st", 2), sems("n_sto", 2), sem("n_zero")

        at = 0
        xt, at = carve(at, R, 2, D)
        xn, at = carve(at, R, 2, D)
        xnT, at = carve(at, 128, 2, KC, 128)
        pqr, at = carve(at, R, 2, 3, D)
        zero, at = carve(at, R, D)
        rows0, at = carve(at, 128, 2, CPT * R)
        rows0 = rows0.bitcast(i32)
        st, at = carve(at, R, 2, 6)
        mv, at = carve(at, R, 2, 2)
        lv, at = carve(at, R, 2, 2)
        dc, at = carve(at, R, CPT)
        dd, at = carve(at, R, CPT)
        mm, at = carve(at, R, CPT)
        hit, at = carve(at, R, 4, R)
        assert at <= 20480

        def rows_of(table, t):
            return table[bass.ds(t * R, R), :]

        with nc.Block() as block:
            @block.sync
            def _(sp):
                for dst_, src_ in ((srcc, src_cols), (dsti, dst_cols)):
                    sp.dma_start(dst_[:, :], src_).then_inc(c_idx, 16)
                sp.dma_start(w1a[:, :, :], W1[0:2 * D, :].rearrange("(k p) n -> p k n", p=128)).then_inc(c_w1, 16)
                sp.dma_start(w3x[:, :, :], W3[0:D, :].rearrange("(k p) n -> p k n", p=128)).then_inc(c_w1, 16)

                def step(c, i):
                    if c < NT or not static(i):
                        need(sp, n_xn, c + 2 * i - 1)
                        sp.dma_start(xt[:, c % 2, :], rows_of(x, c + 2 * i)).then_inc(n_x[c % 2], 16)
                        need(sp, n_dup, (c + 2 * i - 1) * CPT)
                        sp.dma_start(rows0[:, c % 2, :],
                                     dst_row[0:1, bass.ds((c + 2 * i) * (CPT * R), CPT * R)]
                                     .to_broadcast([128, CPT * R])).then_inc(n_row[c % 2], 16)
                    t = c - 2
                    if t >= 0:
                        sp.wait_ge(n_ev, 2 * (t + 2 * i) + 2)
                        sp.wait_ge(n_evp, t + 2 * i + 1)
                        for k, table in enumerate((P_d, Q_d, R_d)):
                            sp.dma_start(rows_of(table, t + 2 * i), pqr[:, t % 2, k, :]).then_inc(n_st[t % 2], 16)
                step(0, 0)
                step(1, 0)
                with sp.Fori(0, (NT - 2) // 2) as i:
                    step(2, i)
                    step(3, i)
                step(NT, 0)
                step(NT + 1, 0)
                for k in range(2):
                    sp.wait_ge(n_st[k], 48 * (NT // 2))
                sp.wait_ge(n_mm, NT)
                sp.dma_start(w3a, W3[D:2 * D, :].rearrange("(k p) n -> p k n", p=128)).then_inc(c_wlate, 16)
                sp.dma_start(w4, W4.rearrange("(k p) n -> p k n", p=128)).then_inc(c_wlate, 16)
                sp.wait_ge(c_wlate, 32)

            @block.gpsimd
            def _(pool):
                pool.memset(ident[:, :], 0.0).then_inc(c_cst, 1)
                pool.memset(before[:, :], 1.0).then_inc(c_cst, 1)
                pool.wait_ge(c_cst, 2)
                pool.affine_select(out=ident[:, :], in_=ident[:, :], compare_op=ALU.not_equal, fill=1.0,
                                   base=0, pattern=[[-1, 128]], channel_multiplier=1).then_inc(c_cst, 1)
                pool.affine_select(out=before[:, :], in_=before[:, :], compare_op=ALU.is_gt, fill=0.0,
                                   base=0, pattern=[[-1, 128]], channel_multiplier=1).then_inc(c_cst, 1)
                pool.iota(dummy[:, :], [[0, 1]], base=NODES, channel_multiplier=1,
                          allow_small_or_imprecise_dtypes=True).then_inc(c_cst, 1)
                pool.iota(iota8[:, :], [[1, TOPK]], base=0, channel_multiplier=0,
                          allow_small_or_imprecise_dtypes=True).then_inc(c_cst, 1)
                pool.memset(eps[:, :], EPS).then_inc(c_cst, 1)
                pool.memset(ln2[:, :], LN2).then_inc(c_cst, 1)
                pool.memset(zero[:, :], 0.0).then_inc(c_cst, 1)
                pool.memset(ones[:, :], 1.0).then_inc(c_cst, 1)

            @block.scalar
            def _(act):
                act.preload_act_table_set(ACT_TABLES)
                row = lambda v: v.rearrange("(a n) -> a n", a=1).to_broadcast([128, D])
                for dst_, v in ((b1b, b1), (b3b, b3)):
                    act.dma_start(dst_[:, :], row(v)).then_inc(c_in, 16)
                for dst_, v in ((b2b, b2), (b4b, b4), (gab, gamma), (beb, beta)):
                    act.dma_start(dst_[:, :], row(v)).then_inc(c_cst2, 16)
                act.dma_start(bqc[:, :], bq_cols).then_inc(c_cst2, 16)
                act.dma_start(w1c[:, :], W1[2 * D:2 * D + EC, :]).then_inc(c_cst2, 16)
                act.dma_start(w2[:, :, :], W2.rearrange("(k p) n -> p k n", p=128)).then_inc(c_cst2, 16)
                act.wait_ge(c_cst, 10)
                for a in agg_d:
                    for k in range(NT + 1):
                        act.dma_start(a[k * R:(k + 1) * R, :], zero[:, :]).then_inc(n_zero, 16)

                def step(c, i):
                    if c < NT or not static(i):
                        s = c % 2
                        act.wait_ge(n_mv, c + 2 * i + 1)
                        act.activation(lv[:, s, 0:1], mv[:, s, 1:2], ACT.Ln, bias=eps[0:R, :]).then_inc(n_lv, 1)
                        act.wait_ge(n_lv, c + 2 * i + 1)
                        act.activation(lv[:, s, 1:2], lv[:, s, 0:1], ACT.Exp, scale=-0.5).then_inc(n_rs, 1)
                    t = c - 2
                    if t >= 0:
                        act.wait_ge(n_mm, t + 2 * i + 1)
                        need(act, n_st[t % 2], 48 * (t // 2 + i))
                        act.activation(pqr[:, t % 2, 0, :], banks[2 + 3 * (t % 2)][0:R, :], ACT.Copy).then_inc(n_evp, 1)
                    if c < NT or not static(i):
                        act.wait_ge(n_T, c + 2 * i + 1)
                        need(act, n_mm, c + 2 * i - 1)
                        act.activation(xnT[:, c % 2, :, 0:R],
                                       banks[c % 2][:, :].rearrange("p (k r) -> p k r", k=KC)[:, :, 0:R],
                                       ACT.Copy).then_inc(n_xt, 1)
                        act.wait_ge(n_xn, c + 2 * i + 1)
                        act.dma_start(rows_of(xn_d, c + 2 * i), xn[:, c % 2, :]).then_inc(n_sto[c % 2], 16)
                step(0, 0)
                step(1, 0)
                with act.Fori(0, (NT - 2) // 2) as i:
                    step(2, i)
                    step(3, i)
                step(NT, 0)
                step(NT + 1, 0)
                act.wait_ge(n_zero, 16 * 2 * (NT + 1))
                act.wait_ge(n_sto[0], 16 * NT // 2)
                act.wait_ge(n_sto[1], 16 * NT // 2)
                act.wait_ge(c_cst2, 16 * 7)

            @block.vector
            def _(dve):
                dve.wait_ge(c_idx, 32)
                dve.tensor_copy(dstf[:, :], dsti[:, :]).then_inc(n_sx, 1)
                dve.wait_ge(n_sx, 1)
                dve.wait_ge(c_cst, 10)
                dve.wait_ge(c_in, 32)

                def step(c, i):
                    n, s = c + 2 * i, c % 2
                    if c < NT or not static(i):
                        dve.wait_ge(n_x[s], 16 * (c // 2 + i + 1))
                        dve.bn_stats(st[:, s, :], xt[:, s, :]).then_inc(n_stat, 1)
                        wait_alone(dve, n_stat, n + 1)
                        dve.bn_aggr(mv[:, s, :], st[:, s, :]).then_inc(n_mv, 1)
                    t = c - 2
                    if t >= 0:
                        dve.wait_ge(n_mm, t + 2 * i + 1)
                        need(dve, n_st[t % 2], 48 * (t // 2 + i))
                        for k, b in ((1, b1b), (2, b3b)):
                            dve.tensor_tensor(pqr[:, t % 2, k, :], banks[2 + 3 * (t % 2) + k][0:R, :], b[0:R, :],
                                              ALU.add).then_inc(n_ev, 1)
                    if c < NT or not static(i):
                        dve.wait_ge(n_rs, n + 1)
                        need(dve, n_T, n - 1)
                        need(dve, n_sto[s], 16 * (c // 2 + i))
                        dve.tensor_scalar(xn[:, s, :], xt[:, s, :], mv[:, s, 0:1], lv[:, s, 1:2],
                                          ALU.subtract, ALU.mult).then_inc(n_xn, 1)
                        dve.tensor_copy(dc[:, :], dstf[:, bass.ds(n * CPT, CPT)]).then_inc(n_dc, 1)
                        dve.wait_ge(n_dc, n + 1)
                        dve.wait_ge(n_row[s], 16 * (c // 2 + i + 1))
                        for k in range(CPT):
                            need(dve, n_dup, n * CPT + k - 3)
                            dve.scalar_tensor_tensor(
                                hit[:, k % 4, :], rows0[0:R, s, k * R:(k + 1) * R], dc[:, k:k + 1], before[0:R, 0:R],
                                ALU.is_equal, ALU.mult, accum_out=cnt[:, bass.ds(n * CPT + k, 1)]).then_inc(n_dup, 1)
                        dve.tensor_scalar(dd[:, :], dc[:, :], -1.0, dummy[:, 0:1], ALU.mult, ALU.add).then_inc(n_dd, 1)
                        dve.wait_ge(n_dup, (n + 1) * CPT)
                        dve.wait_ge(n_dd, n + 1)
                        dve.scalar_tensor_tensor(mm[:, :], cnt[:, bass.ds(n * CPT, CPT)], 0.0, dd[:, :], ALU.is_gt, ALU.mult).then_inc(n_m, 1)
                        dve.wait_ge(n_m, n + 1)
                        dve.tensor_tensor(sidx[:, bass.ds(n * CPT, CPT)], mm[:, :], dc[:, :], ALU.add)\
                           .then_inc(n_sx, 1)
                step(0, 0)
                step(1, 0)
                with dve.Fori(0, (NT - 2) // 2) as i:
                    step(2, i)
                    step(3, i)
                step(NT, 0)
                dve.wait_ge(n_dup, ET)
                dve.tensor_reduce(cnts[:, :], cnt[:, :], AX, ALU.add).then_inc(n_cs, 1)
                step(NT + 1, 0)
                dve.wait_ge(n_any, 1)
                dve.tensor_scalar(shared[:, :], banks[0][0:1, 0:1], 1.0, None, ALU.min).then_inc(n_sh, 1)
                dve.wait_ge(n_sh, 1)

            @block.tensor
            def _(pe):
                pe.wait_ge(c_cst, 10)

                def step(c, i):
                    if c < NT or not static(i):
                        n = c + 2 * i
                        pe.wait_ge(n_xn, n + 1)
                        need(pe, n_xt, n - 1)
                        for k in range(KC):
                            last = pe.transpose(banks[c % 2][:, 128 * k:128 * k + R],
                                                xn[:, c % 2, 128 * k:128 * (k + 1)], ident[0:R, 0:R])
                        last.then_inc(n_T, 1)
                    t = c - 1
                    if t >= 0:
                        pe.wait_ge(n_xt, t + 2 * i + 1)
                        need(pe, n_ev, 2 * (t + 2 * i - 1))
                        need(pe, n_evp, t + 2 * i - 1)
                        for m in range(3):
                            for k in range(KC):
                                w = w1a[:, m * KC + k, :] if m < 2 else w3x[:, k, :]
                                last = pe.matmul(banks[2 + 3 * (t % 2) + m][0:R, :], xnT[:, t % 2, k, 0:R], w,
                                                 start=(k == 0), stop=(k == KC - 1))
                        last.then_inc(n_mm, 1)
                step(0, 0)
                pe.wait_ge(c_w1, 32)
                step(1, 0)
                with pe.Fori(0, (NT - 2) // 2) as i:
                    step(2, i)
                    step(3, i)
                step(NT, 0)
                pe.wait_ge(n_cs, 1)
                pe.wait_ge(n_xt, NT)
                pe.matmul(banks[0][:, 0:1], ones[:, :], cnts[:, :], start=True, stop=True).then_inc(n_any, 1)

        LAG = 4
        PASSES = ET + LAG
        FIRST, LAST = 12, ET - 2
        assert (LAST - FIRST) % 4 == 0
        e_ea, e_row, e_gat = sems("e_ea", 2), sems("e_row", 2), sems("e_gat", 4)
        e_E, e_T, e_W2, e_S = (sem(n) for n in ("e_E", "e_T", "e_W2", "e_S"))
        e_a1, e_pre, e_x2, e_sel = (sem(n) for n in ("e_a1", "e_pre", "e_x2", "e_sel"))
        e_u, e_c, e_v, e_ln, e_r, e_h = (sem(n) for n in ("e_u", "e_c", "e_v", "e_ln", "e_r", "e_h"))
        e_hT, e_ms, e_ix, e_sc, e_sci = sem("e_hT"), sem("e_ms"), sem("e_ix"), sems("e_sc", 2), sem("e_sci")
        e_dcol = sem("e_dcol")
        at = 0
        G, at = carve(at, R, 4, 2, D)
        X, at = carve(at, R, 4, 2 * D)
        U, at = carve(at, R, 2, 2 * D)
        V, at = carve(at, R, 2, 2 * D)
        H, at = carve(at, R, 4, 2 * D)
        hT, at = carve(at, 128, 2, KC, 128)
        sel, at = carve(at, R, 2, R)
        ea, at = carve(at, EC, 2, 2 * R)
        rowb, at = carve(at, 128, 2, 2 * R)
        rowb = rowb.bitcast(i32)
        gix, at = carve(at, R, 4, 2)
        gix = gix.bitcast(i32)
        six, at = carve(at, R, 4, 1)
        six = six.bitcast(i32)
        dcol, at = carve(at, R, 2, 1)
        msum = H[:, 2:4].rearrange("p s (a n) -> p (s a) n", a=2)
        assert at <= 20480
        Eb, Tb, Wb, Sb = banks[0:2], banks[2:4], banks[4:6], banks[6:8]

        def in_range(c, i, lo=0, hi=ET):
            return not static(i) or lo <= c < hi

        def span(c, i):
            if not static(i):
                return 0, 2 * D
            return (0 if c < ET else D), (2 * D if c >= LAG else D)

        def run(eng, step, first=0, last=ET + 9):
            for n in range(first, FIRST):
                step(n, 0)
            with eng.Fori(0, (LAST - FIRST) // 4) as i:
                for c in range(FIRST, FIRST + 4):
                    step(c, i)
            for n in range(LAST, last):
                step(n, 0)

        def edges(plain):
            HS = 4 if plain else 2
            with nc.Block() as block:
                @block.sync
                def _(sp):
                    def load(g, j):
                        if g < ET // 2:
                            need(sp, e_E, 2 * (g + 2 * j) - 2)
                            sp.dma_start(ea[:, g % 2, :], ea_t[:, bass.ds((g + 2 * j) * (2 * R), 2 * R)])\
                              .then_inc(e_ea[g % 2], 16)
                        q = -1 if plain else g - 3
                        if q >= 0:
                            need(sp, e_sel, 2 * (q + 2 * j) - 2)
                            sp.dma_start(rowb[:, q % 2, :],
                                         dst_row[0:1, bass.ds((q + 2 * j) * (2 * R), 2 * R)].to_broadcast([128, 2 * R]))\
                              .then_inc(e_row[q % 2], 16)
                    for g in range(5):
                        load(g, 0)
                    with sp.Fori(0, (ET // 2 - 5) // 2) as j:
                        load(5, j)
                        load(6, j)
                    for g in range(ET // 2, ET // 2 + 3):
                        load(g, 0)

                @block.gpsimd
                def _(pool):
                    def step(c, i):
                        if in_range(c + 2, i):
                            t, k = c + 2, (c + 2) % 4
                            need(pool, e_gat[k], 32 * (t // 4 + i))
                            wait_alone(pool, e_pre, t + 4 * i - 3)
                            pool.tensor_copy(gix[:, k, 0:1], srcc[:, bass.ds(t + 4 * i, 1)]).then_inc(e_ix, 1)
                            pool.tensor_copy(gix[:, k, 1:2], dsti[:, bass.ds(t + 4 * i, 1)]).then_inc(e_ix, 1)
                            wait_alone(pool, e_ix, 2 * (t + 4 * i) + 2)
                            for m, table in enumerate((P_d, Q_d)):
                                pool.indirect_dma_start(
                                    out=G[:, k, m, :], out_offset=None, in_=table,
                                    in_offset=bass.IndirectOffsetOnAxis(ap=gix[:, k, m:m + 1], axis=0),
                                    bounds_check=NODES - 1, oob_is_err=True).then_inc(e_gat[k], 16)
                        back = 8 if plain else 9
                        if in_range(c - back, i):
                            t, k = c - back, (c - back) % 4
                            wait_alone(pool, e_sc[t % 2], 16 * (t // 2 + 2 * i))
                            pool.tensor_copy(six[:, k, :], sidx[:, bass.ds(t + 4 * i, 1)]).then_inc(e_sci, 1)
                            pool.wait_ge(e_sci, t + 4 * i + 1)
                            if plain:
                                wait_alone(pool, e_h, t + 4 * i + LAG + 1)
                            else:
                                wait_alone(pool, e_ms, t + 4 * i + 1)
                            pool.indirect_dma_start(
                                out=agg_d[t % 2], out_offset=bass.IndirectOffsetOnAxis(ap=six[:, k, :], axis=0),
                                in_=H[:, k, D:2 * D] if plain else msum[:, k, :], in_offset=None,
                                bounds_check=NODES + R - 1, oob_is_err=True, compute_op=ALU.add)\
                                .then_inc(e_sc[t % 2], 16)
                    run(pool, step, first=-2)
                    for k in range(2):
                        pool.wait_ge(e_sc[k], 16 * (ET // 2))

                @block.scalar
                def _(act):
                    act.preload_act_table_set(ACT_TABLES)
                    def step(c, i):
                        n = c + 4 * i
                        if in_range(c - 3, i, 0, PASSES):
                            p = c - 3
                            lo, hi = span(p, i)
                            v = V[:, p % 2, lo:hi]
                            act.wait_ge(e_v, n - 2)
                            act.activation(v, v, ACT.Ln, bias=1.0).then_inc(e_ln, 1)
                            act.wait_ge(e_ln, n - 2)
                            act.activation(v, v, ACT.Exp, bias=ln2[0:R, :], scale=-1.0).then_inc(e_r, 1)
                        if in_range(c - 2, i, 0, PASSES):
                            p = c - 2
                            lo, hi = span(p, i)
                            if in_range(p, i):
                                act.wait_ge(e_pre, n - 1)
                            if in_range(p - LAG, i):
                                act.wait_ge(e_x2, n - 1 - LAG)
                            act.activation(U[:, p % 2, lo:hi], X[:, p % 4, lo:hi], ACT.Exp).then_inc(e_u, 1)
                        if in_range(c - 4, i):
                            t = c - 4
                            act.wait_ge(e_T, n - 3)
                            need(act, e_W2, n - 5)
                            act.activation(hT[:, t % 2, :, 0:R],
                                           Tb[t % 2][:, :].rearrange("p (k r) -> p k r", k=KC)[:, :, 0:R],
                                           ACT.Copy).then_inc(e_hT, 1)
                        if not plain and in_range(c - 8, i):
                            t = c - 8
                            act.wait_ge(e_S, n - 7)
                            need(act, e_sc[t % 2], 16 * ((t - 4) // 2 + 2 * i + 1))
                            act.activation(msum[:, t % 4, :], Sb[t % 2][0:R, :], ACT.Copy).then_inc(e_ms, 1)
                        if in_range(c - 2, i, 0, PASSES):
                            p = c - 2
                            lo, hi = span(p, i)
                            act.wait_ge(e_c, n - 1)
                            need(act, e_h, n - 3)
                            act.activation(V[:, p % 2, lo:hi], U[:, p % 2, lo:hi], ACT.Square).then_inc(e_v, 1)
                    run(act, step)

                @block.vector
                def _(dve):
                    def step(c, i):
                        n = c + 4 * i
                        if in_range(c - 6, i):
                            t = c - 6
                            dve.wait_ge(e_W2, n - 5)
                            dve.tensor_tensor(X[:, (t + LAG) % 4, D:2 * D], Wb[t % 2][0:R, :], b2b[0:R, :],
                                              ALU.add).then_inc(e_x2, 1)
                        if in_range(c - 1, i):
                            t = c - 1
                            k = t % 4
                            dve.wait_ge(e_E, n)
                            dve.wait_ge(e_gat[k], 32 * (t // 4 + i + 1))
                            dve.tensor_tensor(X[:, k, 0:D], Eb[t % 2][0:R, :], G[:, k, 0, :], ALU.add).then_inc(e_a1, 1)
                            dve.wait_ge(e_a1, n)
                            dve.tensor_tensor(X[:, k, 0:D], X[:, k, 0:D], G[:, k, 1, :], ALU.add).then_inc(e_pre, 1)
                        if not plain and in_range(c - 7, i):
                            t = c - 7
                            dve.wait_ge(e_row[(t // 2) % 2], 16 * (t // 4 + i + 1))
                            dve.tensor_copy(dcol[:, t % 2, :], dstf[:, bass.ds(t + 4 * i, 1)]).then_inc(e_dcol, 1)
                            dve.wait_ge(e_dcol, n - 6)
                            need(dve, e_S, n - 8)
                            dve.tensor_scalar(sel[:, t % 2, :], rowb[0:R, (t // 2) % 2, (t % 2) * R:(t % 2 + 1) * R],
                                              dcol[:, t % 2, :], None, ALU.is_equal).then_inc(e_sel, 1)
                        if in_range(c - 3, i, 0, PASSES):
                            p = c - 3
                            lo, hi = span(p, i)
                            dve.wait_ge(e_r, n - 2)
                            need(dve, e_T, min(p - HS + 1, ET) if static(i) else n - 2 - HS)
                            if not plain:
                                need(dve, e_S, n - 2 - HS - LAG)
                            elif p >= HS + LAG:
                                dve.wait_ge(e_sc[p % 2], 16 * ((p - HS - LAG) // 2 + 2 * i + 1))
                            dve.scalar_tensor_tensor(H[:, p % HS, lo:hi], V[:, p % 2, lo:hi], 1.0, X[:, p % 4, lo:hi],
                                                     ALU.subtract, ALU.mult, reverse0=True).then_inc(e_h, 1)
                        if in_range(c - 2, i, 0, PASSES):
                            p = c - 2
                            lo, hi = span(p, i)
                            u = U[:, p % 2, lo:hi]
                            dve.wait_ge(e_u, n - 1)
                            dve.tensor_scalar(u, u, UMAX, 1.0, ALU.min, ALU.add).then_inc(e_c, 1)
                    run(dve, step)

                @block.tensor
                def _(pe):
                    def step(c, i):
                        n = c + 4 * i
                        if in_range(c - 4, i):
                            t = c - 4
                            pe.wait_ge(e_h, n - 3)
                            need(pe, e_hT, n - 5)
                            for k in range(KC):
                                last = pe.transpose(Tb[t % 2][:, 128 * k:128 * k + R],
                                                    H[:, t % HS, 128 * k:128 * (k + 1)], ident[0:R, 0:R])
                            last.then_inc(e_T, 1)
                        if not plain and in_range(c - 8, i):
                            t = c - 8
                            pe.wait_ge(e_h, n - 3)
                            pe.wait_ge(e_sel, n - 7)
                            need(pe, e_ms, n - 9)
                            pe.matmul(Sb[t % 2][0:R, :], sel[:, t % 2, :], H[:, t % HS, D:2 * D],
                                      start=True, stop=True).then_inc(e_S, 1)
                        if in_range(c, i):
                            g = (c // 2) % 2
                            pe.wait_ge(e_ea[g], 16 * (c // 4 + i + 1))
                            need(pe, e_pre, n - 1)
                            pe.matmul(Eb[c % 2][0:R, :], ea[:, g, (c % 2) * R:(c % 2 + 1) * R], w1c[:, :],
                                      start=True, stop=True).then_inc(e_E, 1)
                        if in_range(c - 5, i):
                            t = c - 5
                            pe.wait_ge(e_hT, n - 4)
                            need(pe, e_x2, n - 6)
                            for k in range(KC):
                                last = pe.matmul(Wb[t % 2][0:R, :], hT[:, t % 2, k, 0:R], w2[:, k, :],
                                                 start=(k == 0), stop=(k == KC - 1))
                            last.then_inc(e_W2, 1)
                    run(pe, step)

        two_of_a_node = nc.values_load(shared[:, :], min_val=0, max_val=1)
        with nc.If(two_of_a_node == 0):
            edges(True)
        with nc.Else():
            edges(False)

        m_in, m_in2, m_wq = sems("m_in", 2), sems("m_in2", 2), sem("m_wq")
        m_ag, m_T, m_aT, m_3, m_x = (sem(n) for n in ("m_ag", "m_T", "m_aT", "m_3", "m_x"))
        m_u, m_c, m_v, m_ln, m_r, m_h = (sem(n) for n in ("m_u", "m_c", "m_v", "m_ln", "m_r", "m_h"))
        m_T2, m_hT, m_4, m_y1, m_y = (sem(n) for n in ("m_T2", "m_hT", "m_4", "m_y1", "m_y"))
        m_s, m_mv, m_lv, m_rs, m_ch, m_o = (sem(n) for n in ("m_s", "m_mv", "m_lv", "m_rs", "m_ch", "m_o"))
        m_st = sems("m_st", 2)
        at = 0
        A, at = carve(at, R, 2, 3, D)
        XN, at = carve(at, R, 2, 2, D)
        AG, at = carve(at, R, 2, D)
        aT, at = carve(at, 128, 2, KC, 128)
        MX, at = carve(at, R, 4, D)
        MU, at = carve(at, R, 2, D)
        MV, at = carve(at, R, 2, D)
        MH, at = carve(at, R, 2, D)
        hT3, at = carve(at, 128, 2, KC, 128)
        Y, at = carve(at, R, 2, D)
        XO, at = carve(at, R, 2, 2, D)
        sty, at = carve(at, R, 2, 6)
        mvy, at = carve(at, R, 2, 2)
        lvy, at = carve(at, R, 2, 2)
        assert at <= 20480

        def run3(eng, step, last=NT + 3):
            for n in range(4):
                step(n, 0)
            with eng.Fori(0, (NT - 4) // 2) as i:
                step(4, i)
                step(5, i)
            for n in range(NT, last):
                step(n, 0)

        with nc.Block() as block:
            @block.sync
            def _(sp):
                sp.dma_start(wq[:, :, :], Wq.rearrange("(k p) n -> p k n", p=128)).then_inc(m_wq, 16)
                sp.dma_start(keys[:, :], keys_t).then_inc(m_wq, 16)

                def step(c, i):
                    n = c + 2 * i
                    if in_range(c, i, 0, NT):
                        s = c % 2
                        need(sp, m_ag, n - 1)
                        need(sp, m_x, n - 1)
                        for k, table in enumerate((agg_d[0], agg_d[1], R_d)):
                            sp.dma_start(A[:, s, k, :], rows_of(table, n)).then_inc(m_in[s], 16)
                    if in_range(c - 1, i, 0, NT):
                        s = (c - 1) % 2
                        need(sp, m_o, n - 2)
                        sp.dma_start(XN[:, s, 0, :], rows_of(xn_d, n - 1)).then_inc(m_in2[s], 16)
                        sp.dma_start(XN[:, s, 1, :], rows_of(x, n - 1)).then_inc(m_in2[s], 16)
                run3(sp, step)
                sp.wait_ge(m_wq, 32)

            @block.gpsimd
            def _(pool):
                def step(c, i):
                    if in_range(c - 3, i, 0, NT):
                        t = c - 3
                        pool.wait_ge(m_o, c + 2 * i - 2)
                        for k, table in enumerate((x2_d, xf_d)):
                            pool.dma_start(rows_of(table, t + 2 * i), XO[:, t % 2, k, :]).then_inc(m_st[t % 2], 16)
                run3(pool, step)
                for k in range(2):
                    pool.wait_ge(m_st[k], 32 * (NT // 2))

            @block.scalar
            def _(act):
                act.preload_act_table_set(ACT_TABLES)
                def step(c, i):
                    n = c + 2 * i
                    if in_range(c - 3, i, 0, NT):
                        s = (c - 3) % 2
                        act.wait_ge(m_mv, 2 * n - 5)
                        act.activation(lvy[:, s, 0:1], mvy[:, s, 1:2], ACT.Ln, bias=eps[0:R, :]).then_inc(m_lv, 1)
                        act.wait_ge(m_lv, 2 * n - 5)
                        act.activation(lvy[:, s, 1:2], lvy[:, s, 0:1], ACT.Exp, scale=-0.5).then_inc(m_rs, 1)
                    if in_range(c - 1, i, 0, NT):
                        s = (c - 1) % 2
                        act.wait_ge(m_x, n)
                        act.activation(MU[:, s, :], MX[:, s, :], ACT.Exp).then_inc(m_u, 1)
                    if in_range(c, i, 0, NT):
                        s = c % 2
                        act.wait_ge(m_T, n + 1)
                        need(act, m_3, n - 1)
                        act.activation(aT[:, s, :, 0:R],
                                       banks[s][:, :].rearrange("p (k r) -> p k r", k=KC)[:, :, 0:R],
                                       ACT.Copy).then_inc(m_aT, 1)
                    if in_range(c - 1, i, 0, NT):
                        s = (c - 1) % 2
                        act.wait_ge(m_v, n)
                        act.activation(MV[:, s, :], MV[:, s, :], ACT.Ln, bias=1.0).then_inc(m_ln, 1)
                        act.wait_ge(m_ln, n)
                        act.activation(MV[:, s, :], MV[:, s, :], ACT.Exp, bias=ln2[0:R, :], scale=-1.0).then_inc(m_r, 1)
                    if in_range(c - 2, i, 0, NT):
                        s = (c - 2) % 2
                        act.wait_ge(m_T2, n - 1)
                        need(act, m_4, n - 3)
                        act.activation(hT3[:, s, :, 0:R],
                                       banks[4 + s][:, :].rearrange("p (k r) -> p k r", k=KC)[:, :, 0:R],
                                       ACT.Copy).then_inc(m_hT, 1)
                    if in_range(c - 3, i, 0, NT):
                        s = (c - 3) % 2
                        act.wait_ge(m_mv, 2 * n - 4)
                        act.activation(lvy[:, s, 0:1], mvy[:, s, 1:2], ACT.Ln, bias=eps[0:R, :]).then_inc(m_lv, 1)
                        act.wait_ge(m_lv, 2 * n - 4)
                        act.activation(lvy[:, s, 1:2], lvy[:, s, 0:1], ACT.Exp, scale=-0.5).then_inc(m_rs, 1)
                run3(act, step)

            @block.vector
            def _(dve):
                def step(c, i):
                    n = c + 2 * i
                    if in_range(c, i, 0, NT):
                        s = c % 2
                        dve.wait_ge(m_in[s], 48 * (c // 2 + i + 1))
                        need(dve, m_T, n - 1)
                        dve.tensor_tensor(AG[:, s, :], A[:, s, 0, :], A[:, s, 1, :], ALU.add).then_inc(m_ag, 1)
                    if in_range(c - 3, i, 0, NT):
                        s = (c - 3) % 2
                        dve.wait_ge(m_y, n - 2)
                        dve.bn_stats(sty[:, s, :], Y[:, s, :]).then_inc(m_s, 1)
                        wait_alone(dve, m_s, 2 * n - 5)
                        dve.bn_aggr(mvy[:, s, :], sty[:, s, :]).then_inc(m_mv, 1)
                    if in_range(c - 1, i, 0, NT):
                        s = (c - 1) % 2
                        dve.wait_ge(m_u, n)
                        dve.tensor_scalar(MU[:, s, :], MU[:, s, :], UMAX, 1.0, ALU.min, ALU.add).then_inc(m_c, 1)
                        dve.wait_ge(m_c, n)
                        dve.tensor_tensor(MV[:, s, :], MU[:, s, :], MU[:, s, :], ALU.mult).then_inc(m_v, 1)
                    if in_range(c - 3, i, 0, NT):
                        s = (c - 3) % 2
                        q = 4 * (n - 3)
                        x2 = XO[:, s, 0, :]
                        dve.wait_ge(m_rs, 2 * n - 5)
                        need(dve, m_st[s], 32 * ((c - 3) // 2 + i))
                        dve.tensor_scalar(x2, Y[:, s, :], mvy[:, s, 0:1], lvy[:, s, 1:2],
                                          ALU.subtract, ALU.mult).then_inc(m_ch, 1)
                        dve.wait_ge(m_ch, q + 1)
                        dve.tensor_tensor(x2, x2, gab[0:R, :], ALU.mult).then_inc(m_ch, 1)
                        dve.wait_ge(m_ch, q + 2)
                        dve.tensor_tensor(x2, x2, beb[0:R, :], ALU.add).then_inc(m_ch, 1)
                        dve.wait_ge(m_ch, q + 3)
                        dve.tensor_tensor(x2, x2, XN[:, s, 1, :], ALU.add).then_inc(m_ch, 1)
                        dve.wait_ge(m_ch, q + 4)
                        dve.bn_stats(sty[:, s, :], x2).then_inc(m_s, 1)
                        wait_alone(dve, m_s, 2 * n - 4)
                        dve.bn_aggr(mvy[:, s, :], sty[:, s, :]).then_inc(m_mv, 1)
                    if in_range(c - 1, i, 0, NT):
                        s = (c - 1) % 2
                        dve.wait_ge(m_r, n)
                        need(dve, m_T2, n - 2)
                        dve.scalar_tensor_tensor(MH[:, s, :], MV[:, s, :], 1.0, MX[:, s, :],
                                                 ALU.subtract, ALU.mult, reverse0=True).then_inc(m_h, 1)
                    if in_range(c, i, 0, NT):
                        s = c % 2
                        dve.wait_ge(m_3, n + 1)
                        dve.tensor_tensor(MX[:, s, :], banks[2 + s][0:R, :], A[:, s, 2, :], ALU.add).then_inc(m_x, 1)
                    if in_range(c - 3, i, 0, NT):
                        s = (c - 3) % 2
                        dve.wait_ge(m_rs, 2 * n - 4)
                        dve.tensor_scalar(XO[:, s, 1, :], XO[:, s, 0, :], mvy[:, s, 0:1], lvy[:, s, 1:2],
                                          ALU.subtract, ALU.mult).then_inc(m_o, 1)
                    if in_range(c - 2, i, 0, NT):
                        s = (c - 2) % 2
                        dve.wait_ge(m_in2[s], 32 * ((c - 2) // 2 + i + 1))
                        dve.wait_ge(m_4, n - 1)
                        dve.tensor_tensor(Y[:, s, :], banks[6 + s][0:R, :], XN[:, s, 0, :], ALU.add).then_inc(m_y1, 1)
                        dve.wait_ge(m_y1, n - 1)
                        dve.tensor_tensor(Y[:, s, :], Y[:, s, :], b4b[0:R, :], ALU.add).then_inc(m_y, 1)
                run3(dve, step)

            @block.tensor
            def _(pe):
                def step(c, i):
                    n = c + 2 * i
                    if in_range(c - 2, i, 0, NT):
                        s = (c - 2) % 2
                        pe.wait_ge(m_h, n - 1)
                        need(pe, m_hT, n - 3)
                        for k in range(KC):
                            last = pe.transpose(banks[4 + s][:, 128 * k:128 * k + R],
                                                MH[:, s, 128 * k:128 * (k + 1)], ident[0:R, 0:R])
                        last.then_inc(m_T2, 1)
                    if in_range(c, i, 0, NT):
                        s = c % 2
                        pe.wait_ge(m_ag, n + 1)
                        need(pe, m_aT, n - 1)
                        for k in range(KC):
                            last = pe.transpose(banks[s][:, 128 * k:128 * k + R],
                                                AG[:, s, 128 * k:128 * (k + 1)], ident[0:R, 0:R])
                        last.then_inc(m_T, 1)
                    if in_range(c - 2, i, 0, NT):
                        s = (c - 2) % 2
                        pe.wait_ge(m_hT, n - 1)
                        need(pe, m_y1, n - 3)
                        for k in range(KC):
                            last = pe.matmul(banks[6 + s][0:R, :], hT3[:, s, k, 0:R], w4[:, k, :],
                                             start=(k == 0), stop=(k == KC - 1))
                        last.then_inc(m_4, 1)
                    if in_range(c, i, 0, NT):
                        s = c % 2
                        pe.wait_ge(m_aT, n + 1)
                        need(pe, m_x, n - 1)
                        for k in range(KC):
                            last = pe.matmul(banks[2 + s][0:R, :], aT[:, s, k, 0:R], w3a[:, k, :],
                                             start=(k == 0), stop=(k == KC - 1))
                        last.then_inc(m_3, 1)
                run3(pe, step)

        f_xq, f_x, f_x2, f_w, f_out = sem("f_xq"), sems("f_x", 2), sems("f_x2", 2), sems("f_w", RING), sems("f_out", 2)
        f_T, f_xT, f_q, f_qs, f_s = (sem(n) for n in ("f_T", "f_xT", "f_q", "f_qs", "f_s"))
        f_m, f_top, f_fin, f_e, f_idx = (sem(n) for n in ("f_m", "f_top", "f_fin", "f_e", "f_idx"))
        f_in, f_val, f_dg, f_pe, f_o = (sem(n) for n in ("f_in", "f_val", "f_dg", "f_pe", "f_o"))
        f_m2, f_rc, f_prob = sem("f_m2"), sem("f_rc"), sem("f_prob")
        NW = RING * 2 * D
        ring = wide[0:R, 0:NW].rearrange("p (j n) -> p j n", j=RING)
        at = NW
        xq, at = carve(at, R, D)
        xqT, at = carve(at, 128, KC, 128)
        qh, at = carve(at, 128, 2, 128)
        obuf, at = carve(at, R, 2, D)
        assert at <= 20480
        spare = w1a[0:R, :, :].rearrange("p k n -> p (k n)")
        xc = spare[:, 0:2 * D].rearrange("p (s n) -> p s n", s=2)
        xr = spare[:, 2 * D:4 * D].rearrange("p (s n) -> p s n", s=2)
        junk = spare[:, 4 * D:8 * D].rearrange("p (s n) -> p s n", s=4)
        spare2 = w2[0:R, :, :].rearrange("p k n -> p (k n)")
        at2 = 0

        def small(n, dt=f32):
            nonlocal at2
            v = spare2[:, at2:at2 + n]
            at2 += n
            return v if dt is f32 else v.bitcast(dt)

        top = small(2 * PICKS).rearrange("p (h a k) -> p h a k", h=HEADS, a=2)
        topi = small(2 * PICKS, u32).rearrange("p (h a k) -> p h a k", h=HEADS, a=2)
        topf = small(2 * PICKS).rearrange("p (h a k) -> p h a k", h=HEADS, a=2)
        best = small(PICKS).rearrange("p (h k) -> p h k", h=HEADS)
        pos = small(PICKS, u32).rearrange("p (h k) -> p h k", h=HEADS)
        posi = small(PICKS, u32).rearrange("p (h k) -> p h k", h=HEADS)
        posj = small(PICKS, u32).rearrange("p (h k) -> p h k", h=HEADS)
        hi_f = small(PICKS).rearrange("p (h k) -> p h k", h=HEADS)
        lo_f = small(PICKS).rearrange("p (h k) -> p h k", h=HEADS)
        ex = small(PICKS).rearrange("p (h k) -> p h k", h=HEADS)
        es = small(HEADS)
        er = small(HEADS)
        prob = small(2 * PICKS).rearrange("p (s h k) -> p s h k", s=2, h=HEADS)
        idx = small(2 * PICKS, i32).rearrange("p (s j) -> p s j", s=2)
        inner = small(2 * TOPK).rearrange("p (s k) -> p s k", s=2)
        vals = small(2 * TOPK).rearrange("p (s k) -> p s k", s=2)
        spare3 = w3x[0:R, :, :].rearrange("p k n -> p (k n)")
        dg = spare3[:, 0:8 * 128].rearrange("p (s n) -> p s n", s=8)
        comb = spare3[:, 2 * D:3 * D]
        eq = spare3[:, 3 * D:4 * D]
        FIN = 11
        DSLOTS = 8

        with nc.Block() as block:
            @block.sync
            def _(sp):
                sp.dma_start(xq, rows_of(xf_d, 0)).then_inc(f_xq, 16)
                sp.wait_ge(f_T, 1)
                sp.dma_start(xq, rows_of(xf_d, 1)).then_inc(f_xq, 16)
                for s in range(2):
                    sp.dma_start(xc[:, s, :], rows_of(xf_d, s)).then_inc(f_x[s], 16)
                    sp.dma_start(xr[:, s, :], rows_of(x2_d, s)).then_inc(f_x2[s], 16)

                def tile(s, t, more):
                    if more:
                        sp.wait_ge(f_T, t + 2)
                        sp.dma_start(xq, rows_of(xf_d, t + 2)).then_inc(f_xq, 16)
                    sp.wait_ge(f_o, t + 1)
                    sp.dma_start(rows_of(out, t), obuf[:, s, :]).then_inc(f_out[s], 16)
                with sp.Fori(0, NT // 2 - 1) as i:
                    for s in range(2):
                        t = 2 * i + s
                        tile(s, t, True)
                        sp.dma_start(xc[:, s, :], rows_of(xf_d, t + 2)).then_inc(f_x[s], 16)
                        sp.dma_start(xr[:, s, :], rows_of(x2_d, t + 2)).then_inc(f_x2[s], 16)
                tile(0, NT - 2, False)
                tile(1, NT - 1, False)
                for s in range(2):
                    sp.wait_ge(f_out[s], 16 * (NT // 2))

            @block.gpsimd
            def _(pool):
                def tile(s, t, more):
                    wait_alone(pool, f_idx, t + 1)
                    for j in range(PICKS):
                        k = j % RING
                        if not isinstance(t, int) or t * PICKS + j >= RING:
                            wait_alone(pool, f_pe, t * PICKS + j - RING + 1)
                        pool.indirect_dma_start(
                            out=ring[:, k, :], out_offset=None, in_=w_du,
                            in_offset=bass.IndirectOffsetOnAxis(ap=idx[:, s, j:j + 1], axis=0),
                            bounds_check=NKEYS * NKEYS - 1, oob_is_err=True).then_inc(f_w[k], 16)

                tile(0, 0, True)
                tile(1, 1, True)
                with pool.Fori(1, NT // 2) as i:
                    tile(0, 2 * i, True)
                    tile(1, 2 * i + 1, True)

            @block.scalar
            def _(act):
                act.preload_act_table_set(ACT_TABLES)
                def look_up_head(tq, h):
                    q = tq * HEADS + h
                    act.wait_ge(f_q, q + 1)
                    need(act, f_s, q - 1) if isinstance(q, int) else act.wait_ge(f_s, q - 1)
                    act.activation(qh[:, h % 2, 0:R], banks[3][:, 0:R], ACT.Identity,
                                   bias=bqc[:, h:h + 1]).then_inc(f_qs, 1)

                def transposed(tq):
                    act.wait_ge(f_T, tq + 1)
                    act.activation(xqT[:, :, 0:R],
                                   banks[2][:, :].rearrange("p (k r) -> p k r", k=KC)[:, :, 0:R],
                                   ACT.Copy).then_inc(f_xT, 1)

                def exps(tq):
                    act.wait_ge(f_fin, tq * FIN + 2)
                    act.activation(ex, ex, ACT.Exp).then_inc(f_e, 1)

                transposed(0)
                for h in range(HEADS):
                    look_up_head(0, h)
                exps(0)

                def tile(s, t, more):
                    if more:
                        transposed(t + 1)
                    for h in range(HEADS):
                        if more and h < 4:
                            look_up_head(t + 1, 2 * h)
                            look_up_head(t + 1, 2 * h + 1)
                        act.wait_ge(f_val, t * HEADS + h + 1)
                        for k in range(TOPK):
                            j = h * TOPK + k
                            if not isinstance(t, int) or t * PICKS + j >= DSLOTS:
                                act.wait_ge(f_pe, t * PICKS + j - DSLOTS + 1)
                            act.activation(dg[:, j % DSLOTS, 0:R], ident[0:R, 0:R], ACT.Copy,
                                           scale=vals[:, h % 2, k:k + 1]).then_inc(f_dg, 1)
                        if more and h == 4:
                            exps(t + 1)
                tile(0, 0, True)
                with act.Fori(0, NT // 2 - 1) as i:
                    tile(1, 2 * i + 1, True)
                    tile(0, 2 * i + 2, True)
                tile(1, NT - 1, False)

            @block.vector
            def _(dve):
                def look_up_head(tq, h):
                    q = tq * HEADS + h
                    wait_alone(dve, f_s, q + 1)
                    for a in range(2):
                        sc = banks[4 + 2 * (h % 2) + a][0:R, 0:NKEYS]
                        dve.max(out=top[:, h, a, :], in_=sc).then_inc(f_m, 1)
                    for a in range(2):
                        sc = banks[4 + 2 * (h % 2) + a][0:R, 0:NKEYS]
                        wait_alone(dve, f_m, 2 * q + a + 1)
                        last = dve.max_index(topi[:, h, a, :], top[:, h, a, :], sc)
                    last.then_inc(f_top, 1)

                H3 = [R, HEADS, TOPK, TOPK]
                comb4 = comb.rearrange("p (h i j) -> p h i j", h=HEADS, i=TOPK)
                eq4 = eq.rearrange("p (h i j) -> p h i j", h=HEADS, i=TOPK)

                def finish(tq, s):
                    n = [0]

                    def link(ins):
                        n[0] += 1
                        ins.then_inc(f_fin, 1)
                        wait_alone(dve, f_fin, tq * FIN + n[0])
                    dve.wait_ge(f_top, tq * HEADS + HEADS)
                    dve.tensor_copy(topf, topi)
                    link(dve.tensor_tensor(comb4, top[:, :, 0, :].unsqueeze(3).to_broadcast(H3),
                                           top[:, :, 1, :].unsqueeze(2).to_broadcast(H3), ALU.add))
                    for h in range(HEADS):
                        last = dve.max(out=best[:, h, :], in_=comb[:, 64 * h:64 * (h + 1)])
                    last.then_inc(f_m2, 1)
                    wait_alone(dve, f_m2, tq + 1)
                    link(dve.tensor_tensor(ex, best, best[:, :, 0:1].to_broadcast([R, HEADS, TOPK]), ALU.subtract))
                    for h in range(HEADS):
                        last = dve.max_index(pos[:, h, :], best[:, h, :], comb[:, 64 * h:64 * (h + 1)])
                    link(last)
                    dve.tensor_scalar(posi, pos, 3, None, ALU.logical_shift_right)
                    link(dve.tensor_scalar(posj, pos, TOPK - 1, None, ALU.bitwise_and))
                    for pp, a, res in ((posi, 0, hi_f), (posj, 1, lo_f)):
                        link(dve.tensor_tensor(eq4, pp.unsqueeze(3).to_broadcast(H3),
                                               iota8[:, :].unsqueeze(1).unsqueeze(1).to_broadcast(H3), ALU.is_equal))
                        link(dve.tensor_tensor(eq4, eq4, topf[:, :, a, :].unsqueeze(2).to_broadcast(H3), ALU.mult))
                        link(dve.tensor_reduce(res, eq4, AX, ALU.add))
                    dve.scalar_tensor_tensor(idx[:, s, :], hi_f.rearrange("p h k -> p (h k)"), float(NKEYS),
                                             lo_f.rearrange("p h k -> p (h k)"), ALU.mult, ALU.add).then_inc(f_idx, 1)
                    dve.wait_ge(f_e, tq + 1)
                    link(dve.tensor_reduce(es, ex, AX, ALU.add))
                    dve.reciprocal(er, es).then_inc(f_rc, 1)
                    dve.wait_ge(f_rc, tq + 1)
                    dve.tensor_tensor(prob[:, s], ex, er.unsqueeze(2).to_broadcast([R, HEADS, TOPK]), ALU.mult)\
                       .then_inc(f_prob, 1)
                    assert n[0] == FIN

                dve.wait_ge(c_cst, 10)
                for h in range(HEADS):
                    look_up_head(0, h)
                finish(0, 0)

                def tile(s, t, more, i):
                    dve.wait_ge(f_x[s], 16 * (i + 1))
                    dve.wait_ge(f_prob, t + 1)
                    for h in range(HEADS):
                        for k in range(TOPK):
                            j = h * TOPK + k
                            dve.wait_ge(f_w[j % RING], 16 * (t * (PICKS // RING) + j // RING + 1))
                            need(dve, f_in, t * PICKS + j - 3)
                            dve.scalar_tensor_tensor(junk[:, j % 4, :], ring[:, j % RING, 0:D], 1.0, xc[:, s, :],
                                                            ALU.mult, ALU.mult, accum_out=inner[:, h % 2, k:k + 1])\
                               .then_inc(f_in, 1)
                        dve.wait_ge(f_in, t * PICKS + (h + 1) * TOPK)
                        if not isinstance(t, int) or t * HEADS + h >= 2:
                            dve.wait_ge(f_dg, (t * HEADS + h - 1) * TOPK)
                        dve.scalar_tensor_tensor(vals[:, h % 2, :], inner[:, h % 2, :], 0.0, prob[:, s, h, :],
                                                 ALU.max, ALU.mult).then_inc(f_val, 1)
                        if more and h < 4:
                            look_up_head(t + 1, 2 * h)
                            look_up_head(t + 1, 2 * h + 1)
                        if more and h == 4:
                            finish(t + 1, 1 - s)
                    dve.wait_ge(f_x2[s], 16 * (i + 1))
                    dve.wait_ge(f_pe, (t + 1) * PICKS)
                    if not isinstance(i, int) or i > 0:
                        dve.wait_ge(f_out[s], 16 * i)
                    dve.tensor_tensor(obuf[:, s, :], banks[s][0:R, :], xr[:, s, :], ALU.add).then_inc(f_o, 1)
                tile(0, 0, True, 0)
                with dve.Fori(0, NT // 2 - 1) as i:
                    tile(1, 2 * i + 1, True, i)
                    tile(0, 2 * i + 2, True, i + 1)
                tile(1, NT - 1, False, NT // 2 - 1)

            @block.tensor
            def _(pe):
                def transposed(tq):
                    pe.wait_ge(f_xq, 16 * (tq + 1))
                    for k in range(KC):
                        last = pe.transpose(banks[2][:, 128 * k:128 * k + R], xq[:, 128 * k:128 * (k + 1)],
                                            ident[0:R, 0:R])
                    last.then_inc(f_T, 1)

                def queries(tq, h):
                    q = tq * HEADS + h
                    pe.wait_ge(f_xT, tq + 1)
                    if not isinstance(q, int) or q > 0:
                        pe.wait_ge(f_qs, q)
                    for k in range(KC):
                        last = pe.matmul(banks[3][:, 0:R], wq[:, k, 128 * h:128 * (h + 1)], xqT[:, k, 0:R],
                                         start=(k == 0), stop=(k == KC - 1))
                    last.then_inc(f_q, 1)

                def scores(tq, h):
                    q = tq * HEADS + h
                    pe.wait_ge(f_qs, q + 1)
                    if not isinstance(q, int) or q > 1:
                        pe.wait_ge(f_top, q - 1)
                    for a in range(2):
                        half = slice(HALF * a, HALF * (a + 1))
                        last = pe.matmul(banks[4 + 2 * (h % 2) + a][0:R, 0:NKEYS], qh[half, h % 2, 0:R],
                                         keys[half, NKEYS * h:NKEYS * (h + 1)], start=True, stop=True)
                    last.then_inc(f_s, 1)

                transposed(0)
                for h in range(HEADS):
                    queries(0, h)
                    scores(0, h)

                def tile(s, t, more):
                    if more:
                        transposed(t + 1)
                    for h in range(HEADS):
                        if more and h < 4:
                            for g in (2 * h, 2 * h + 1):
                                queries(t + 1, g)
                                scores(t + 1, g)
                        for k in range(TOPK):
                            j = h * TOPK + k
                            pe.wait_ge(f_dg, t * PICKS + j + 1)
                            if j == 0 and (not isinstance(t, int) or t >= 2):
                                pe.wait_ge(f_o, t - 1)
                            pe.matmul(banks[s][0:R, :], dg[:, j % DSLOTS, 0:R], ring[:, j % RING, D:2 * D],
                                      start=(j == 0), stop=(j == PICKS - 1)).then_inc(f_pe, 1)
                tile(0, 0, True)
                tile(1, 1, True)
                with pe.Fori(1, NT // 2 - 1) as i:
                    tile(0, 2 * i, True)
                    tile(1, 2 * i + 1, True)
                tile(0, NT - 2, True)
                tile(1, NT - 1, False)


def kernel(**inputs):
    import numpy as np
    import concourse.bacc as bacc
    from concourse import mybir as mb
    from concourse.bass_utils import run_bass_kernel_spmd

    a = {k: np.asarray(v) for k, v in inputs.items()}
    rows = 125
    src, dst, ea = a["src"], a["dst"], a["edge_attr_64"]
    keys = a["L0_ffn_keys"]
    heads, halves, n_keys, width = keys.shape
    laid = {
        "x": a["x"],
        "src_cols": src.reshape(rows, -1),
        "dst_cols": dst.reshape(rows, -1),
        "dst_row": dst.reshape(rows, -1).T.reshape(1, -1),
        "ea_t": ea.reshape(rows, -1, ea.shape[1]).transpose(2, 1, 0).reshape(ea.shape[1], -1),
        **{n: a[f"L0_gnn_{n}"] for n in ("W1", "b1", "W2", "b2", "W3", "b3", "W4", "b4", "gamma", "beta")},
        "Wq": a["L0_ffn_Wq"],
        "bq_cols": a["L0_ffn_bq"].reshape(heads, -1).T,
        "keys_t": keys.transpose(1, 3, 0, 2).reshape(halves * width, heads * n_keys),
        "w_du": np.concatenate([a["L0_ffn_w_down"], a["L0_ffn_w_up"]], axis=1),
    }
    nc = bacc.Bacc("TRN2", target_bir_lowering=False, num_devices=1)
    arrays, args = {}, []
    for name, v in laid.items():
        v = np.ascontiguousarray(v)
        arrays[f"in_{name}"] = v
        args.append(nc.dram_tensor(f"in_{name}", v.shape, mb.dt.from_np(v.dtype), kind="ExternalInput").ap())
    out = nc.dram_tensor("out_0", a["x"].shape, mb.dt.float32, kind="ExternalOutput").ap()
    gnn_peer_kernel(nc, *args, out)
    r = run_bass_kernel_spmd(nc, [arrays], core_ids=[0])
    return r.results[0]["out_0"]
```

```python
import concourse.bass as bass
from concourse import mybir
from contextlib import ExitStack


def gnn_peer_kernel(nc, x, src_cols, dst_cols, dst_row, ea_t, W1, b1, W2, b2, W3, b3, W4, b4,
                    gamma, beta, Wq, bq_cols, keys_t, w_du, out):
    f32 = mybir.dt.float32
    i32, u32 = mybir.dt.int32, mybir.dt.uint32
    ALU = mybir.AluOpType
    ACT = mybir.ActivationFunctionType
    AX = mybir.AxisListType.X

    NODES, D = x.shape
    EC, EDGES = ea_t.shape
    R = src_cols.shape[0]
    NT = NODES // R
    ET = EDGES // R
    KC = D // 128
    HEADS, TOPK = 8, 8
    HALF = keys_t.shape[0] // 2
    NKEYS = keys_t.shape[1] // HEADS
    PICKS = HEADS * TOPK
    CPT = ET // NT
    EPS = 1e-5
    LN2 = 0.6931471805599453
    ACT_TABLES = "natural_log_exp_and_others"
    UMAX = 1e9
    WIDE = 28960
    RING = 16
    assert NT * R == NODES and ET * R == EDGES and CPT * NT == ET and NT % 2 == 0

    ctx = ExitStack()
    with ctx:
        def sb(name, shape, dt=f32):
            return ctx.enter_context(nc.sbuf_tensor(name, shape, dt))

        def sem(name):
            return ctx.enter_context(nc.semaphore(name))

        def sems(name, n):
            return [sem(f"{name}{k}") for k in range(n)]

        def static(i):
            return isinstance(i, int)

        def need(eng, s, value):
            if not isinstance(value, int) or value > 0:
                eng.wait_ge(s, value)

        def wait_alone(eng, s, value):
            need(eng, s, value)
            if not isinstance(value, int):
                eng.sem_inc(passed, 1)

        P_d = nc.dram_tensor("P_d", (NODES, D), f32, kind="Internal").ap()
        Q_d = nc.dram_tensor("Q_d", (NODES, D), f32, kind="Internal").ap()
        R_d = nc.dram_tensor("R_d", (NODES, D), f32, kind="Internal").ap()
        xn_d = nc.dram_tensor("xn_d", (NODES, D), f32, kind="Internal").ap()
        agg_d = [nc.dram_tensor(f"agg{k}_d", (NODES + R, D), f32, kind="Internal").ap() for k in range(2)]

        ident = sb("ident", [128, 128])
        before = sb("before", [128, 128])
        srcc = sb("srcc", [R, ET], i32)
        dsti = sb("dsti", [R, ET], i32)
        dstf = sb("dstf", [R, ET])
        sidx = sb("sidx", [R, ET], i32)
        dummy = sb("dummy_row", [R, 1])
        ones = sb("ones", [R, 128])
        cnt = sb("cnt", [R, ET])
        cnts = sb("cnts", [R, 1])
        shared = sb("shared", [1, 1], i32)
        eps = sb("eps", [128, 1])
        ln2 = sb("ln2", [128, 1])
        b1b, b2b, b3b, b4b = (sb(n, [128, D]) for n in ("b1b", "b2b", "b3b", "b4b"))
        gab, beb = sb("gab", [128, D]), sb("beb", [128, D])
        bqc = sb("bqc", [128, HEADS])
        iota8 = sb("iota8", [R, TOPK])
        w1a = sb("w1a", [128, 2 * KC, D])
        w1c = sb("w1c", [EC, D])
        w2 = sb("w2", [128, KC, D])
        w3x = sb("w3x", [128, KC, D])
        wide = sb("wide", [128, WIDE])
        wq = sb("wq", [128, KC, HEADS * 128])
        keys = sb("keys", [128, HEADS * NKEYS])
        banks = [ctx.enter_context(nc.psum_tensor(f"bank{k}", [128, 512], f32)) for k in range(8)]
        w3a, w4 = w1a[:, 0:KC, :], w1a[:, KC:2 * KC, :]

        def carve(at, rows, *dims):
            n = 1
            for d in dims:
                n *= d
            v = wide[0:rows, at:at + n]
            if len(dims) == 2:
                v = v.rearrange("p (a b) -> p a b", a=dims[0])
            elif len(dims) == 3:
                v = v.rearrange("p (a b c) -> p a b c", a=dims[0], b=dims[1])
            return v, at + n

        c_in, c_w1, c_w3, c_cst, c_cst2 = sem("c_in"), sem("c_w1"), sem("c_w3"), sem("c_cst"), sem("c_cst2")
        passed = sem("passed")
        c_idx, c_wlate = sem("c_idx"), sem("c_wlate")
        n_x, n_row = sems("n_x", 2), sems("n_row", 2)
        n_stat, n_mv, n_lv, n_rs, n_xn = (sem(n) for n in ("n_stat", "n_mv", "n_lv", "n_rs", "n_xn"))
        n_T, n_xt, n_mm, n_ev, n_evp = (sem(n) for n in ("n_T", "n_xt", "n_mm", "n_ev", "n_evp"))
        n_dc, n_dup, n_dd, n_m, n_sx = (sem(n) for n in ("n_dc", "n_dup", "n_dd", "n_m", "n_sx"))
        n_cs, n_any, n_sh = sem("n_cs"), sem("n_any"), sem("n_sh")
        n_st, n_sto, n_zero = sems("n_st", 2), sems("n_sto", 2), sem("n_zero")

        at = 0
        xt, at = carve(at, R, 2, D)
        xn, at = carve(at, R, 2, D)
        xnT, at = carve(at, 128, 2, KC, 128)
        pqr, at = carve(at, R, 2, 3, D)
        zero, at = carve(at, R, D)
        rows0, at = carve(at, 128, 2, CPT * R)
        rows0 = rows0.bitcast(i32)
        st, at = carve(at, R, 2, 6)
        mv, at = carve(at, R, 2, 2)
        lv, at = carve(at, R, 2, 2)
        dc, at = carve(at, R, CPT)
        dd, at = carve(at, R, CPT)
        mm, at = carve(at, R, CPT)
        hit, at = carve(at, R, 4, R)
        assert at <= WIDE

        def rows_of(table, t):
            return table[bass.ds(t * R, R), :]

        with nc.Block() as block:
            @block.sync
            def _(sp):
                for dst_, src_ in ((srcc, src_cols), (dsti, dst_cols)):
                    sp.dma_start(dst_[:, :], src_).then_inc(c_idx, 16)
                sp.dma_start(w1a[:, :, :], W1[0:2 * D, :].rearrange("(k p) n -> p k n", p=128)).then_inc(c_w1, 16)
                sp.dma_start(w3x[:, :, :], W3[0:D, :].rearrange("(k p) n -> p k n", p=128)).then_inc(c_w1, 16)

                def step(c, i):
                    if c < NT or not static(i):
                        need(sp, n_xn, c + 2 * i - 1)
                        sp.dma_start(xt[:, c % 2, :], rows_of(x, c + 2 * i)).then_inc(n_x[c % 2], 16)
                        need(sp, n_dup, (c + 2 * i - 1) * CPT)
                        sp.dma_start(rows0[:, c % 2, :],
                                     dst_row[0:1, bass.ds((c + 2 * i) * (CPT * R), CPT * R)]
                                     .to_broadcast([128, CPT * R])).then_inc(n_row[c % 2], 16)
                    t = c - 2
                    if t >= 0:
                        sp.wait_ge(n_ev, 2 * (t + 2 * i) + 2)
                        sp.wait_ge(n_evp, t + 2 * i + 1)
                        for k, table in enumerate((P_d, Q_d, R_d)):
                            sp.dma_start(rows_of(table, t + 2 * i), pqr[:, t % 2, k, :]).then_inc(n_st[t % 2], 16)
                step(0, 0)
                step(1, 0)
                with sp.Fori(0, (NT - 2) // 2) as i:
                    step(2, i)
                    step(3, i)
                step(NT, 0)
                step(NT + 1, 0)
                for k in range(2):
                    sp.wait_ge(n_st[k], 48 * (NT // 2))
                sp.wait_ge(n_mm, NT)
                sp.dma_start(w3a, W3[D:2 * D, :].rearrange("(k p) n -> p k n", p=128)).then_inc(c_wlate, 16)
                sp.dma_start(w4, W4.rearrange("(k p) n -> p k n", p=128)).then_inc(c_wlate, 16)
                sp.dma_start(wq[:, :, :], Wq.rearrange("(k p) n -> p k n", p=128)).then_inc(c_wlate, 16)
                sp.dma_start(keys[:, :], keys_t).then_inc(c_wlate, 16)

            @block.gpsimd
            def _(pool):
                pool.memset(ident[:, :], 0.0).then_inc(c_cst, 1)
                pool.memset(before[:, :], 1.0).then_inc(c_cst, 1)
                pool.wait_ge(c_cst, 2)
                pool.affine_select(out=ident[:, :], in_=ident[:, :], compare_op=ALU.not_equal, fill=1.0,
                                   base=0, pattern=[[-1, 128]], channel_multiplier=1).then_inc(c_cst, 1)
                pool.affine_select(out=before[:, :], in_=before[:, :], compare_op=ALU.is_gt, fill=0.0,
                                   base=0, pattern=[[-1, 128]], channel_multiplier=1).then_inc(c_cst, 1)
                pool.iota(dummy[:, :], [[0, 1]], base=NODES, channel_multiplier=1,
                          allow_small_or_imprecise_dtypes=True).then_inc(c_cst, 1)
                pool.iota(iota8[:, :], [[1, TOPK]], base=0, channel_multiplier=0,
                          allow_small_or_imprecise_dtypes=True).then_inc(c_cst, 1)
                pool.memset(eps[:, :], EPS).then_inc(c_cst, 1)
                pool.memset(ln2[:, :], LN2).then_inc(c_cst, 1)
                pool.memset(zero[:, :], 0.0).then_inc(c_cst, 1)
                pool.memset(ones[:, :], 1.0).then_inc(c_cst, 1)

            @block.scalar
            def _(act):
                act.preload_act_table_set(ACT_TABLES)
                row = lambda v: v.rearrange("(a n) -> a n", a=1).to_broadcast([128, D])
                for dst_, v in ((b1b, b1), (b3b, b3)):
                    act.dma_start(dst_[:, :], row(v)).then_inc(c_in, 16)
                for dst_, v in ((b2b, b2), (b4b, b4), (gab, gamma), (beb, beta)):
                    act.dma_start(dst_[:, :], row(v)).then_inc(c_cst2, 16)
                act.dma_start(bqc[:, :], bq_cols).then_inc(c_cst2, 16)
                act.dma_start(w1c[:, :], W1[2 * D:2 * D + EC, :]).then_inc(c_cst2, 16)
                act.dma_start(w2[:, :, :], W2.rearrange("(k p) n -> p k n", p=128)).then_inc(c_cst2, 16)
                act.wait_ge(c_cst, 10)
                for a in agg_d:
                    for k in range(NT + 1):
                        act.dma_start(a[k * R:(k + 1) * R, :], zero[:, :]).then_inc(n_zero, 16)

                def step(c, i):
                    if c < NT or not static(i):
                        s = c % 2
                        act.wait_ge(n_mv, c + 2 * i + 1)
                        act.activation(lv[:, s, 0:1], mv[:, s, 1:2], ACT.Ln, bias=eps[0:R, :]).then_inc(n_lv, 1)
                        act.wait_ge(n_lv, c + 2 * i + 1)
                        act.activation(lv[:, s, 1:2], lv[:, s, 0:1], ACT.Exp, scale=-0.5).then_inc(n_rs, 1)
                    t = c - 2
                    if t >= 0:
                        act.wait_ge(n_mm, t + 2 * i + 1)
                        need(act, n_st[t % 2], 48 * (t // 2 + i))
                        act.activation(pqr[:, t % 2, 0, :], banks[2 + 3 * (t % 2)][0:R, :], ACT.Copy).then_inc(n_evp, 1)
                    if c < NT or not static(i):
                        act.wait_ge(n_T, c + 2 * i + 1)
                        need(act, n_mm, c + 2 * i - 1)
                        act.activation(xnT[:, c % 2, :, 0:R],
                                       banks[c % 2][:, :].rearrange("p (k r) -> p k r", k=KC)[:, :, 0:R],
                                       ACT.Copy).then_inc(n_xt, 1)
                        act.wait_ge(n_xn, c + 2 * i + 1)
                        act.dma_start(rows_of(xn_d, c + 2 * i), xn[:, c % 2, :]).then_inc(n_sto[c % 2], 16)
                step(0, 0)
                step(1, 0)
                with act.Fori(0, (NT - 2) // 2) as i:
                    step(2, i)
                    step(3, i)
                step(NT, 0)
                step(NT + 1, 0)
                act.wait_ge(n_zero, 16 * 2 * (NT + 1))
                act.wait_ge(n_sto[0], 16 * NT // 2)
                act.wait_ge(n_sto[1], 16 * NT // 2)
                act.wait_ge(c_cst2, 16 * 7)

            @block.vector
            def _(dve):
                dve.wait_ge(c_idx, 32)
                dve.tensor_copy(dstf[:, :], dsti[:, :]).then_inc(n_sx, 1)
                dve.wait_ge(n_sx, 1)
                dve.wait_ge(c_cst, 10)
                dve.wait_ge(c_in, 32)

                def step(c, i):
                    n, s = c + 2 * i, c % 2
                    if c < NT or not static(i):
                        dve.wait_ge(n_x[s], 16 * (c // 2 + i + 1))
                        dve.bn_stats(st[:, s, :], xt[:, s, :]).then_inc(n_stat, 1)
                        wait_alone(dve, n_stat, n + 1)
                        dve.bn_aggr(mv[:, s, :], st[:, s, :]).then_inc(n_mv, 1)
                    t = c - 2
                    if t >= 0:
                        dve.wait_ge(n_mm, t + 2 * i + 1)
                        need(dve, n_st[t % 2], 48 * (t // 2 + i))
                        for k, b in ((1, b1b), (2, b3b)):
                            dve.tensor_tensor(pqr[:, t % 2, k, :], banks[2 + 3 * (t % 2) + k][0:R, :], b[0:R, :],
                                              ALU.add).then_inc(n_ev, 1)
                    if c < NT or not static(i):
                        dve.wait_ge(n_rs, n + 1)
                        need(dve, n_T, n - 1)
                        need(dve, n_sto[s], 16 * (c // 2 + i))
                        dve.tensor_scalar(xn[:, s, :], xt[:, s, :], mv[:, s, 0:1], lv[:, s, 1:2],
                                          ALU.subtract, ALU.mult).then_inc(n_xn, 1)
                        dve.tensor_copy(dc[:, :], dstf[:, bass.ds(n * CPT, CPT)]).then_inc(n_dc, 1)
                        dve.wait_ge(n_dc, n + 1)
                        dve.wait_ge(n_row[s], 16 * (c // 2 + i + 1))
                        for k in range(CPT):
                            need(dve, n_dup, n * CPT + k - 3)
                            dve.scalar_tensor_tensor(
                                hit[:, k % 4, :], rows0[0:R, s, k * R:(k + 1) * R], dc[:, k:k + 1], before[0:R, 0:R],
                                ALU.is_equal, ALU.mult, accum_out=cnt[:, bass.ds(n * CPT + k, 1)]).then_inc(n_dup, 1)
                        dve.tensor_scalar(dd[:, :], dc[:, :], -1.0, dummy[:, 0:1], ALU.mult, ALU.add).then_inc(n_dd, 1)
                        dve.wait_ge(n_dup, (n + 1) * CPT)
                        dve.wait_ge(n_dd, n + 1)
                        dve.scalar_tensor_tensor(mm[:, :], cnt[:, bass.ds(n * CPT, CPT)], 0.0, dd[:, :], ALU.is_gt, ALU.mult).then_inc(n_m, 1)
                        dve.wait_ge(n_m, n + 1)
                        dve.tensor_tensor(sidx[:, bass.ds(n * CPT, CPT)], mm[:, :], dc[:, :], ALU.add)\
                           .then_inc(n_sx, 1)
                step(0, 0)
                step(1, 0)
                with dve.Fori(0, (NT - 2) // 2) as i:
                    step(2, i)
                    step(3, i)
                step(NT, 0)
                dve.wait_ge(n_dup, ET)
                dve.tensor_reduce(cnts[:, :], cnt[:, :], AX, ALU.add).then_inc(n_cs, 1)
                step(NT + 1, 0)
                dve.wait_ge(n_any, 1)
                dve.tensor_scalar(shared[:, :], banks[0][0:1, 0:1], 1.0, None, ALU.min).then_inc(n_sh, 1)
                dve.wait_ge(n_sh, 1)

            @block.tensor
            def _(pe):
                pe.wait_ge(c_cst, 10)

                def step(c, i):
                    if c < NT or not static(i):
                        n = c + 2 * i
                        pe.wait_ge(n_xn, n + 1)
                        need(pe, n_xt, n - 1)
                        for k in range(KC):
                            last = pe.transpose(banks[c % 2][:, 128 * k:128 * k + R],
                                                xn[:, c % 2, 128 * k:128 * (k + 1)], ident[0:R, 0:R])
                        last.then_inc(n_T, 1)
                    t = c - 1
                    if t >= 0:
                        pe.wait_ge(n_xt, t + 2 * i + 1)
                        need(pe, n_ev, 2 * (t + 2 * i - 1))
                        need(pe, n_evp, t + 2 * i - 1)
                        for m in range(3):
                            for k in range(KC):
                                w = w1a[:, m * KC + k, :] if m < 2 else w3x[:, k, :]
                                last = pe.matmul(banks[2 + 3 * (t % 2) + m][0:R, :], xnT[:, t % 2, k, 0:R], w,
                                                 start=(k == 0), stop=(k == KC - 1))
                        last.then_inc(n_mm, 1)
                step(0, 0)
                pe.wait_ge(c_w1, 32)
                step(1, 0)
                with pe.Fori(0, (NT - 2) // 2) as i:
                    step(2, i)
                    step(3, i)
                step(NT, 0)
                pe.wait_ge(n_cs, 1)
                pe.wait_ge(n_xt, NT)
                pe.matmul(banks[0][:, 0:1], ones[:, :], cnts[:, :], start=True, stop=True).then_inc(n_any, 1)

        LAG = 4
        PASSES = ET + LAG
        FIRST, LAST = 12, ET - 2
        assert (LAST - FIRST) % 4 == 0
        e_ea, e_row, e_gat = sems("e_ea", 2), sems("e_row", 2), sems("e_gat", 4)
        e_E, e_T, e_W2, e_S = (sem(n) for n in ("e_E", "e_T", "e_W2", "e_S"))
        e_a1, e_pre, e_x2, e_sel = (sem(n) for n in ("e_a1", "e_pre", "e_x2", "e_sel"))
        e_u, e_c, e_v, e_ln, e_r, e_h = (sem(n) for n in ("e_u", "e_c", "e_v", "e_ln", "e_r", "e_h"))
        e_hT, e_ms, e_ix, e_sc, e_sci = sem("e_hT"), sem("e_ms"), sem("e_ix"), sems("e_sc", 2), sem("e_sci")
        e_dcol = sem("e_dcol")
        at = 0
        G, at = carve(at, R, 4, 2, D)
        X, at = carve(at, R, 4, 2 * D)
        U, at = carve(at, R, 2, 2 * D)
        V, at = carve(at, R, 2, 2 * D)
        H, at = carve(at, R, 4, 2 * D)
        hT, at = carve(at, 128, 2, KC, 128)
        sel, at = carve(at, R, 2, R)
        ea, at = carve(at, EC, 2, 2 * R)
        rowb, at = carve(at, 128, 2, 2 * R)
        rowb = rowb.bitcast(i32)
        gix, at = carve(at, R, 4, 2)
        gix = gix.bitcast(i32)
        six, at = carve(at, R, 4, 1)
        six = six.bitcast(i32)
        dcol, at = carve(at, R, 2, 1)
        msum = H[:, 2:4].rearrange("p s (a n) -> p (s a) n", a=2)
        assert at <= WIDE
        Eb, Tb, Wb, Sb = banks[0:2], banks[2:4], banks[4:6], banks[6:8]

        def in_range(c, i, lo=0, hi=ET):
            return not static(i) or lo <= c < hi

        def span(c, i):
            if not static(i):
                return 0, 2 * D
            return (0 if c < ET else D), (2 * D if c >= LAG else D)

        def run(eng, step, first=0, last=ET + 9):
            for n in range(first, FIRST):
                step(n, 0)
            with eng.Fori(0, (LAST - FIRST) // 4) as i:
                for c in range(FIRST, FIRST + 4):
                    step(c, i)
            for n in range(LAST, last):
                step(n, 0)

        def edges(plain):
            HS = 4 if plain else 2
            with nc.Block() as block:
                @block.sync
                def _(sp):
                    def load(g, j):
                        if g < ET // 2:
                            need(sp, e_E, 2 * (g + 2 * j) - 2)
                            sp.dma_start(ea[:, g % 2, :], ea_t[:, bass.ds((g + 2 * j) * (2 * R), 2 * R)])\
                              .then_inc(e_ea[g % 2], 16)
                        q = -1 if plain else g - 3
                        if q >= 0:
                            need(sp, e_sel, 2 * (q + 2 * j) - 2)
                            sp.dma_start(rowb[:, q % 2, :],
                                         dst_row[0:1, bass.ds((q + 2 * j) * (2 * R), 2 * R)].to_broadcast([128, 2 * R]))\
                              .then_inc(e_row[q % 2], 16)
                    for g in range(5):
                        load(g, 0)
                    with sp.Fori(0, (ET // 2 - 5) // 2) as j:
                        load(5, j)
                        load(6, j)
                    for g in range(ET // 2, ET // 2 + 3):
                        load(g, 0)

                @block.gpsimd
                def _(pool):
                    def step(c, i):
                        if in_range(c + 2, i):
                            t, k = c + 2, (c + 2) % 4
                            need(pool, e_gat[k], 32 * (t // 4 + i))
                            wait_alone(pool, e_pre, t + 4 * i - 3)
                            pool.tensor_copy(gix[:, k, 0:1], srcc[:, bass.ds(t + 4 * i, 1)]).then_inc(e_ix, 1)
                            pool.tensor_copy(gix[:, k, 1:2], dsti[:, bass.ds(t + 4 * i, 1)]).then_inc(e_ix, 1)
                            wait_alone(pool, e_ix, 2 * (t + 4 * i) + 2)
                            for m, table in enumerate((P_d, Q_d)):
                                pool.indirect_dma_start(
                                    out=G[:, k, m, :], out_offset=None, in_=table,
                                    in_offset=bass.IndirectOffsetOnAxis(ap=gix[:, k, m:m + 1], axis=0),
                                    bounds_check=NODES - 1, oob_is_err=True).then_inc(e_gat[k], 16)
                        back = 8 if plain else 9
                        if in_range(c - back, i):
                            t, k = c - back, (c - back) % 4
                            wait_alone(pool, e_sc[t % 2], 16 * (t // 2 + 2 * i))
                            pool.tensor_copy(six[:, k, :], sidx[:, bass.ds(t + 4 * i, 1)]).then_inc(e_sci, 1)
                            pool.wait_ge(e_sci, t + 4 * i + 1)
                            if plain:
                                wait_alone(pool, e_h, t + 4 * i + LAG + 1)
                            else:
                                wait_alone(pool, e_ms, t + 4 * i + 1)
                            pool.indirect_dma_start(
                                out=agg_d[t % 2], out_offset=bass.IndirectOffsetOnAxis(ap=six[:, k, :], axis=0),
                                in_=H[:, k, D:2 * D] if plain else msum[:, k, :], in_offset=None,
                                bounds_check=NODES + R - 1, oob_is_err=True, compute_op=ALU.add)\
                                .then_inc(e_sc[t % 2], 16)
                    run(pool, step, first=-2)
                    for k in range(2):
                        pool.wait_ge(e_sc[k], 16 * (ET // 2))

                @block.scalar
                def _(act):
                    act.preload_act_table_set(ACT_TABLES)
                    def step(c, i):
                        n = c + 4 * i
                        if in_range(c - 3, i, 0, PASSES):
                            p = c - 3
                            lo, hi = span(p, i)
                            v = V[:, p % 2, lo:hi]
                            act.wait_ge(e_v, n - 2)
                            act.activation(v, v, ACT.Ln, bias=1.0).then_inc(e_ln, 1)
                        if in_range(c - 2, i, 0, PASSES):
                            p = c - 2
                            lo, hi = span(p, i)
                            if in_range(p, i):
                                act.wait_ge(e_pre, n - 1)
                            if in_range(p - LAG, i):
                                act.wait_ge(e_x2, n - 1 - LAG)
                            act.activation(U[:, p % 2, lo:hi], X[:, p % 4, lo:hi], ACT.Exp).then_inc(e_u, 1)
                        if in_range(c - 3, i, 0, PASSES):
                            act.wait_ge(e_ln, n - 2)
                            act.activation(v, v, ACT.Exp, bias=ln2[0:R, :], scale=-1.0).then_inc(e_r, 1)
                        if in_range(c - 2, i, 0, PASSES):
                            p = c - 2
                            lo, hi = span(p, i)
                            act.wait_ge(e_c, n - 1)
                            need(act, e_h, n - 3)
                            act.activation(V[:, p % 2, lo:hi], U[:, p % 2, lo:hi], ACT.Square).then_inc(e_v, 1)
                        if in_range(c - 4, i):
                            t = c - 4
                            act.wait_ge(e_T, n - 3)
                            need(act, e_W2, n - 5)
                            act.activation(hT[:, t % 2, :, 0:R],
                                           Tb[t % 2][:, :].rearrange("p (k r) -> p k r", k=KC)[:, :, 0:R],
                                           ACT.Copy).then_inc(e_hT, 1)
                        if not plain and in_range(c - 8, i):
                            t = c - 8
                            act.wait_ge(e_S, n - 7)
                            need(act, e_sc[t % 2], 16 * ((t - 4) // 2 + 2 * i + 1))
                            act.activation(msum[:, t % 4, :], Sb[t % 2][0:R, :], ACT.Copy).then_inc(e_ms, 1)
                    run(act, step)

                @block.vector
                def _(dve):
                    def step(c, i):
                        n = c + 4 * i
                        if in_range(c - 6, i):
                            t = c - 6
                            dve.wait_ge(e_W2, n - 5)
                            dve.tensor_tensor(X[:, (t + LAG) % 4, D:2 * D], Wb[t % 2][0:R, :], b2b[0:R, :],
                                              ALU.add).then_inc(e_x2, 1)
                        if in_range(c - 1, i):
                            t = c - 1
                            k = t % 4
                            dve.wait_ge(e_E, n)
                            dve.wait_ge(e_gat[k], 32 * (t // 4 + i + 1))
                            dve.tensor_tensor(X[:, k, 0:D], Eb[t % 2][0:R, :], G[:, k, 0, :], ALU.add).then_inc(e_a1, 1)
                            dve.wait_ge(e_a1, n)
                            dve.tensor_tensor(X[:, k, 0:D], X[:, k, 0:D], G[:, k, 1, :], ALU.add).then_inc(e_pre, 1)
                        if not plain and in_range(c - 7, i):
                            t = c - 7
                            dve.wait_ge(e_row[(t // 2) % 2], 16 * (t // 4 + i + 1))
                            dve.tensor_copy(dcol[:, t % 2, :], dstf[:, bass.ds(t + 4 * i, 1)]).then_inc(e_dcol, 1)
                            dve.wait_ge(e_dcol, n - 6)
                            need(dve, e_S, n - 8)
                            dve.tensor_scalar(sel[:, t % 2, :], rowb[0:R, (t // 2) % 2, (t % 2) * R:(t % 2 + 1) * R],
                                              dcol[:, t % 2, :], None, ALU.is_equal).then_inc(e_sel, 1)
                        if in_range(c - 2, i, 0, PASSES):
                            p = c - 2
                            lo, hi = span(p, i)
                            u = U[:, p % 2, lo:hi]
                            dve.wait_ge(e_u, n - 1)
                            dve.tensor_scalar(u, u, UMAX, 1.0, ALU.min, ALU.add).then_inc(e_c, 1)
                        if in_range(c - 3, i, 0, PASSES):
                            p = c - 3
                            lo, hi = span(p, i)
                            dve.wait_ge(e_r, n - 2)
                            need(dve, e_T, min(p - HS + 1, ET) if static(i) else n - 2 - HS)
                            if not plain:
                                need(dve, e_S, n - 2 - HS - LAG)
                            elif p >= HS + LAG:
                                dve.wait_ge(e_sc[p % 2], 16 * ((p - HS - LAG) // 2 + 2 * i + 1))
                            dve.scalar_tensor_tensor(H[:, p % HS, lo:hi], V[:, p % 2, lo:hi], 1.0, X[:, p % 4, lo:hi],
                                                     ALU.subtract, ALU.mult, reverse0=True).then_inc(e_h, 1)
                    run(dve, step)

                @block.tensor
                def _(pe):
                    def step(c, i):
                        n = c + 4 * i
                        if in_range(c - 4, i):
                            t = c - 4
                            pe.wait_ge(e_h, n - 3)
                            need(pe, e_hT, n - 5)
                            for k in range(KC):
                                last = pe.transpose(Tb[t % 2][:, 128 * k:128 * k + R],
                                                    H[:, t % HS, 128 * k:128 * (k + 1)], ident[0:R, 0:R])
                            last.then_inc(e_T, 1)
                        if not plain and in_range(c - 8, i):
                            t = c - 8
                            pe.wait_ge(e_h, n - 3)
                            pe.wait_ge(e_sel, n - 7)
                            need(pe, e_ms, n - 9)
                            pe.matmul(Sb[t % 2][0:R, :], sel[:, t % 2, :], H[:, t % HS, D:2 * D],
                                      start=True, stop=True).then_inc(e_S, 1)
                        if in_range(c, i):
                            g = (c // 2) % 2
                            pe.wait_ge(e_ea[g], 16 * (c // 4 + i + 1))
                            need(pe, e_pre, n - 1)
                            pe.matmul(Eb[c % 2][0:R, :], ea[:, g, (c % 2) * R:(c % 2 + 1) * R], w1c[:, :],
                                      start=True, stop=True).then_inc(e_E, 1)
                        if in_range(c - 5, i):
                            t = c - 5
                            pe.wait_ge(e_hT, n - 4)
                            need(pe, e_x2, n - 6)
                            for k in range(KC):
                                last = pe.matmul(Wb[t % 2][0:R, :], hT[:, t % 2, k, 0:R], w2[:, k, :],
                                                 start=(k == 0), stop=(k == KC - 1))
                            last.then_inc(e_W2, 1)
                    run(pe, step)

        two_of_a_node = nc.values_load(shared[:, :], min_val=0, max_val=1)
        with nc.If(two_of_a_node == 0):
            edges(True)
        with nc.Else():
            edges(False)

        m_in, m_in2 = sem("m_in"), sem("m_in2")
        m_ag, m_T, m_aT, m_3, m_x = (sem(n) for n in ("m_ag", "m_T", "m_aT", "m_3", "m_x"))
        m_u, m_c, m_v, m_ln, m_r, m_h = (sem(n) for n in ("m_u", "m_c", "m_v", "m_ln", "m_r", "m_h"))
        m_T2, m_hT, m_4, m_y1, m_y = (sem(n) for n in ("m_T2", "m_hT", "m_4", "m_y1", "m_y"))
        m_s, m_mv, m_lv, m_rs, m_ch, m_xf = (sem(n) for n in ("m_s", "m_mv", "m_lv", "m_rs", "m_ch", "m_xf"))
        f_w, f_out = sems("f_w", RING), sems("f_out", 2)
        f_T, f_xT, f_q, f_qs, f_s = (sem(n) for n in ("f_T", "f_xT", "f_q", "f_qs", "f_s"))
        f_m, f_top, f_fin, f_e, f_idx = (sem(n) for n in ("f_m", "f_top", "f_fin", "f_e", "f_idx"))
        f_in, f_val, f_dg, f_pe, f_o = (sem(n) for n in ("f_in", "f_val", "f_dg", "f_pe", "f_o"))
        f_m2, f_rc, f_prob, f_xc, f_xr = (sem(n) for n in ("f_m2", "f_rc", "f_prob", "f_xc", "f_xr"))
        at = 0
        ring, at = carve(at, R, RING, 2 * D)
        A, at = carve(at, R, 3, D)
        XN, at = carve(at, R, 2, D)
        AG, at = carve(at, R, D)
        aT, at = carve(at, 128, KC, 128)
        MX, at = carve(at, R, D)
        MU, at = carve(at, R, D)
        MV, at = carve(at, R, D)
        MH, at = carve(at, R, D)
        hT3, at = carve(at, 128, KC, 128)
        Y, at = carve(at, R, D)
        x2n, at = carve(at, R, D)
        xfn, at = carve(at, R, D)
        xqT, at = carve(at, 128, KC, 128)
        qh, at = carve(at, 128, 2, 128)
        xc, at = carve(at, R, 2, D)
        xr, at = carve(at, R, 2, D)
        sty, at = carve(at, R, 6)
        mvy, at = carve(at, R, 2)
        lvy, at = carve(at, R, 2)
        junk, at = carve(at, R, 4, D)
        assert at <= WIDE
        spare2 = w2[0:R, :, :].rearrange("p k n -> p (k n)")
        at2 = 0

        def small(n, dt=f32):
            nonlocal at2
            v = spare2[:, at2:at2 + n]
            at2 += n
            return v if dt is f32 else v.bitcast(dt)

        top = small(2 * PICKS).rearrange("p (h a k) -> p h a k", h=HEADS, a=2)
        topi = small(2 * PICKS, u32).rearrange("p (h a k) -> p h a k", h=HEADS, a=2)
        topf = small(2 * PICKS).rearrange("p (h a k) -> p h a k", h=HEADS, a=2)
        best = small(PICKS).rearrange("p (h k) -> p h k", h=HEADS)
        pos = small(PICKS, u32).rearrange("p (h k) -> p h k", h=HEADS)
        posi = small(PICKS, u32).rearrange("p (h k) -> p h k", h=HEADS)
        posj = small(PICKS, u32).rearrange("p (h k) -> p h k", h=HEADS)
        hi_f = small(PICKS).rearrange("p (h k) -> p h k", h=HEADS)
        lo_f = small(PICKS).rearrange("p (h k) -> p h k", h=HEADS)
        ex = small(PICKS).rearrange("p (h k) -> p h k", h=HEADS)
        es = small(HEADS)
        er = small(HEADS)
        prob = small(2 * PICKS).rearrange("p (s h k) -> p s h k", s=2, h=HEADS)
        idx = small(2 * PICKS, i32).rearrange("p (s j) -> p s j", s=2)
        inner = small(2 * TOPK).rearrange("p (s k) -> p s k", s=2)
        vals = small(2 * TOPK).rearrange("p (s k) -> p s k", s=2)
        spare3 = w3x[0:R, :, :].rearrange("p k n -> p (k n)")
        dg = spare3[:, 0:8 * 128].rearrange("p (s n) -> p s n", s=8)
        comb = spare3[:, 2 * D:3 * D]
        eq = spare3[:, 3 * D:4 * D]
        FIN = 11
        DSLOTS = 8
        q_bank = (banks[7], banks[4])
        s_bank = banks[5:7]
        by_chunk = lambda bank: bank[:, :].rearrange("p (k r) -> p k r", k=KC)[:, :, 0:R]

        def run_tiles(eng, tile):
            tile(0, 0, True, True)
            tile(1, 0, True, True)
            with eng.Fori(1, NT // 2 - 1) as i:
                tile(0, i, True, True)
                tile(1, i, True, True)
            tile(0, NT // 2 - 1, True, False)
            tile(1, NT // 2 - 1, False, False)

        with nc.Block() as block:
            @block.sync
            def _(sp):
                def load(u):
                    need(sp, m_ag, u)
                    need(sp, m_x, u)
                    for k, table in enumerate((agg_d[0], agg_d[1], R_d)):
                        sp.dma_start(A[:, k, :], rows_of(table, u)).then_inc(m_in, 16)
                    need(sp, m_ch, 4 * u)
                    for k, table in enumerate((xn_d, x)):
                        sp.dma_start(XN[:, k, :], rows_of(table, u)).then_inc(m_in2, 16)
                load(0)
                load(1)

                def tile(s, i, look, node):
                    t = 2 * i + s
                    if node:
                        load(t + 2)
                    sp.wait_ge(f_o, t + 1)
                    sp.dma_start(rows_of(out, t), xr[:, s, :]).then_inc(f_out[s], 16)
                run_tiles(sp, tile)
                for s in range(2):
                    sp.wait_ge(f_out[s], 16 * (NT // 2))

            @block.gpsimd
            def _(pool):
                def tile(s, i, look, node):
                    t = 2 * i + s
                    wait_alone(pool, f_idx, t + 1)
                    for j in range(PICKS):
                        k = j % RING
                        if not static(t) or t * PICKS + j >= RING:
                            wait_alone(pool, f_pe, t * PICKS + j - RING + 1)
                        pool.indirect_dma_start(
                            out=ring[:, k, :], out_offset=None, in_=w_du,
                            in_offset=bass.IndirectOffsetOnAxis(ap=idx[:, s, j:j + 1], axis=0),
                            bounds_check=NKEYS * NKEYS - 1, oob_is_err=True).then_inc(f_w[k], 16)
                run_tiles(pool, tile)

            @block.scalar
            def _(act):
                act.preload_act_table_set(ACT_TABLES)

                def node_agg(u):
                    act.wait_ge(m_T, u + 1)
                    need(act, m_3, u)
                    act.activation(aT[:, :, 0:R], by_chunk(banks[2]), ACT.Copy).then_inc(m_aT, 1)

                def node_exp(u):
                    act.wait_ge(m_x, u + 1)
                    act.activation(MU, MX, ACT.Exp).then_inc(m_u, 1)

                def node_log(u):
                    act.wait_ge(m_c, u + 1)
                    need(act, m_h, u)
                    act.activation(MV, MU, ACT.Square).then_inc(m_v, 1)
                    act.wait_ge(m_v, u + 1)
                    act.activation(MV, MV, ACT.Ln, bias=1.0).then_inc(m_ln, 1)
                    act.wait_ge(m_ln, u + 1)
                    act.activation(MV, MV, ACT.Exp, bias=ln2[0:R, :], scale=-1.0).then_inc(m_r, 1)

                def node_h(u):
                    act.wait_ge(m_T2, u + 1)
                    need(act, m_4, u)
                    act.activation(hT3[:, :, 0:R], by_chunk(banks[2]), ACT.Copy).then_inc(m_hT, 1)

                def node_norm(u, m):
                    act.wait_ge(m_mv, 2 * u + m + 1)
                    act.activation(lvy[:, 0:1], mvy[:, 1:2], ACT.Ln, bias=eps[0:R, :]).then_inc(m_lv, 1)
                    act.wait_ge(m_lv, 2 * u + m + 1)
                    act.activation(lvy[:, 1:2], lvy[:, 0:1], ACT.Exp, scale=-0.5).then_inc(m_rs, 1)

                def look_up_head(tq, h):
                    q = tq * HEADS + h
                    act.wait_ge(f_q, q + 1)
                    need(act, f_s, 2 * (q - 1))
                    act.activation(qh[:, h % 2, 0:R], q_bank[h % 2][:, 0:R], ACT.Identity,
                                   bias=bqc[:, h:h + 1]).then_inc(f_qs, 1)

                def transposed(tq):
                    act.wait_ge(f_T, tq + 1)
                    act.activation(xqT[:, :, 0:R], by_chunk(banks[4]), ACT.Copy).then_inc(f_xT, 1)

                def keep_xf(tq, s):
                    act.wait_ge(m_xf, tq + 1)
                    need(act, f_in, (tq - 1) * PICKS)
                    act.activation(xc[:, s, :], xfn, ACT.Copy).then_inc(f_xc, 1)

                def keep_x2(tq, s, stored):
                    need(act, f_out[s], 16 * stored)
                    act.activation(xr[:, s, :], x2n, ACT.Copy).then_inc(f_xr, 1)

                def exps(tq):
                    act.wait_ge(f_fin, tq * FIN + 2)
                    act.activation(ex, ex, ACT.Exp).then_inc(f_e, 1)

                def node_all(u):
                    node_agg(u)
                    node_exp(u)
                    node_log(u)
                    node_h(u)
                    node_norm(u, 0)
                    node_norm(u, 1)

                node_all(0)
                transposed(0)
                for h in range(HEADS):
                    look_up_head(0, h)
                    if h == 2:
                        keep_xf(0, 0)
                    if h == 4:
                        keep_x2(0, 0, 0)
                exps(0)
                node_all(1)

                def tile(s, i, look, node):
                    t = 2 * i + s
                    for h in range(HEADS):
                        if look and h == 0:
                            transposed(t + 1)
                            keep_xf(t + 1, 1 - s)
                        if node and h == 1:
                            node_agg(t + 2)
                        if look and h < 4:
                            look_up_head(t + 1, 2 * h)
                            look_up_head(t + 1, 2 * h + 1)
                        if look and h == 2:
                            keep_x2(t + 1, 1 - s, i + s)
                        if node:
                            if h == 2:
                                node_exp(t + 2)
                            if h == 3:
                                node_log(t + 2)
                            if h == 4:
                                node_h(t + 2)
                            if h in (5, 6):
                                node_norm(t + 2, h - 5)
                        act.wait_ge(f_val, t * HEADS + h + 1)
                        for k in range(TOPK):
                            j = h * TOPK + k
                            if not static(t) or t * PICKS + j >= DSLOTS:
                                act.wait_ge(f_pe, t * PICKS + j - DSLOTS + 1)
                            act.activation(dg[:, j % DSLOTS, 0:R], ident[0:R, 0:R], ACT.Copy,
                                           scale=vals[:, h % 2, k:k + 1]).then_inc(f_dg, 1)
                        if look and h == 4:
                            exps(t + 1)
                run_tiles(act, tile)

            @block.vector
            def _(dve):
                def node_sum(u):
                    dve.wait_ge(m_in, 48 * (u + 1))
                    need(dve, m_T, u)
                    dve.tensor_tensor(AG, A[:, 0, :], A[:, 1, :], ALU.add).then_inc(m_ag, 1)

                def node_x(u):
                    dve.wait_ge(m_3, u + 1)
                    dve.tensor_tensor(MX, banks[3][0:R, :], A[:, 2, :], ALU.add).then_inc(m_x, 1)

                def node_clamp(u):
                    dve.wait_ge(m_u, u + 1)
                    dve.tensor_scalar(MU, MU, UMAX, 1.0, ALU.min, ALU.add).then_inc(m_c, 1)

                def node_mish(u):
                    dve.wait_ge(m_r, u + 1)
                    need(dve, m_T2, u)
                    dve.scalar_tensor_tensor(MH, MV, 1.0, MX, ALU.subtract, ALU.mult, reverse0=True).then_inc(m_h, 1)

                def node_y(u):
                    dve.wait_ge(m_in2, 32 * (u + 1))
                    dve.wait_ge(m_4, u + 1)
                    dve.tensor_tensor(Y, banks[3][0:R, :], XN[:, 0, :], ALU.add).then_inc(m_y1, 1)
                    dve.wait_ge(m_y1, u + 1)
                    dve.tensor_tensor(Y, Y, b4b[0:R, :], ALU.add).then_inc(m_y, 1)
                    dve.wait_ge(m_y, u + 1)
                    dve.bn_stats(sty, Y).then_inc(m_s, 1)
                    wait_alone(dve, m_s, 2 * u + 1)
                    dve.bn_aggr(mvy, sty).then_inc(m_mv, 1)

                def node_x2(u):
                    dve.wait_ge(m_rs, 2 * u + 1)
                    need(dve, f_xr, u)
                    dve.tensor_scalar(x2n, Y, mvy[:, 0:1], lvy[:, 1:2], ALU.subtract, ALU.mult).then_inc(m_ch, 1)
                    for k, other in enumerate((gab[0:R, :], beb[0:R, :], XN[:, 1, :])):
                        dve.wait_ge(m_ch, 4 * u + 1 + k)
                        dve.tensor_tensor(x2n, x2n, other, ALU.add if k else ALU.mult).then_inc(m_ch, 1)
                    dve.wait_ge(m_ch, 4 * u + 4)
                    dve.bn_stats(sty, x2n).then_inc(m_s, 1)
                    wait_alone(dve, m_s, 2 * u + 2)
                    dve.bn_aggr(mvy, sty).then_inc(m_mv, 1)

                def node_xf(u):
                    dve.wait_ge(m_rs, 2 * u + 2)
                    need(dve, f_T, u)
                    need(dve, f_xc, u)
                    dve.tensor_scalar(xfn, x2n, mvy[:, 0:1], lvy[:, 1:2], ALU.subtract, ALU.mult).then_inc(m_xf, 1)

                def node_all(u):
                    for part in (node_sum, node_x, node_clamp, node_mish, node_y, node_x2, node_xf):
                        part(u)

                def look_up_head(tq, h):
                    q = tq * HEADS + h
                    wait_alone(dve, f_s, 2 * q + 2)
                    for a in range(2):
                        sc = s_bank[h % 2][0:R, NKEYS * a:NKEYS * (a + 1)]
                        dve.max(out=top[:, h, a, :], in_=sc).then_inc(f_m, 1)
                    for a in range(2):
                        sc = s_bank[h % 2][0:R, NKEYS * a:NKEYS * (a + 1)]
                        wait_alone(dve, f_m, 2 * q + a + 1)
                        last = dve.max_index(topi[:, h, a, :], top[:, h, a, :], sc)
                    last.then_inc(f_top, 1)

                H3 = [R, HEADS, TOPK, TOPK]
                comb4 = comb.rearrange("p (h i j) -> p h i j", h=HEADS, i=TOPK)
                eq4 = eq.rearrange("p (h i j) -> p h i j", h=HEADS, i=TOPK)

                def finish(tq, s):
                    n = [0]

                    def link(ins):
                        n[0] += 1
                        ins.then_inc(f_fin, 1)
                        wait_alone(dve, f_fin, tq * FIN + n[0])
                    dve.wait_ge(f_top, tq * HEADS + HEADS)
                    dve.tensor_copy(topf, topi)
                    link(dve.tensor_tensor(comb4, top[:, :, 0, :].unsqueeze(3).to_broadcast(H3),
                                           top[:, :, 1, :].unsqueeze(2).to_broadcast(H3), ALU.add))
                    for h in range(HEADS):
                        last = dve.max(out=best[:, h, :], in_=comb[:, 64 * h:64 * (h + 1)])
                    last.then_inc(f_m2, 1)
                    wait_alone(dve, f_m2, tq + 1)
                    link(dve.tensor_tensor(ex, best, best[:, :, 0:1].to_broadcast([R, HEADS, TOPK]), ALU.subtract))
                    for h in range(HEADS):
                        last = dve.max_index(pos[:, h, :], best[:, h, :], comb[:, 64 * h:64 * (h + 1)])
                    link(last)
                    dve.tensor_scalar(posi, pos, 3, None, ALU.logical_shift_right)
                    link(dve.tensor_scalar(posj, pos, TOPK - 1, None, ALU.bitwise_and))
                    for pp, a, res in ((posi, 0, hi_f), (posj, 1, lo_f)):
                        link(dve.tensor_tensor(eq4, pp.unsqueeze(3).to_broadcast(H3),
                                               iota8[:, :].unsqueeze(1).unsqueeze(1).to_broadcast(H3), ALU.is_equal))
                        link(dve.tensor_tensor(eq4, eq4, topf[:, :, a, :].unsqueeze(2).to_broadcast(H3), ALU.mult))
                        link(dve.tensor_reduce(res, eq4, AX, ALU.add))
                    dve.scalar_tensor_tensor(idx[:, s, :], hi_f.rearrange("p h k -> p (h k)"), float(NKEYS),
                                             lo_f.rearrange("p h k -> p (h k)"), ALU.mult, ALU.add).then_inc(f_idx, 1)
                    dve.wait_ge(f_e, tq + 1)
                    link(dve.tensor_reduce(es, ex, AX, ALU.add))
                    dve.reciprocal(er, es).then_inc(f_rc, 1)
                    dve.wait_ge(f_rc, tq + 1)
                    dve.tensor_tensor(prob[:, s], ex, er.unsqueeze(2).to_broadcast([R, HEADS, TOPK]), ALU.mult)\
                       .then_inc(f_prob, 1)
                    assert n[0] == FIN

                dve.wait_ge(c_cst, 10)
                node_all(0)
                for h in range(HEADS):
                    look_up_head(0, h)
                finish(0, 0)
                node_all(1)

                def tile(s, i, look, node):
                    t = 2 * i + s
                    dve.wait_ge(f_xc, t + 1)
                    dve.wait_ge(f_prob, t + 1)
                    for h in range(HEADS):
                        for k in range(TOPK):
                            j = h * TOPK + k
                            dve.wait_ge(f_w[j % RING], 16 * (t * (PICKS // RING) + j // RING + 1))
                            need(dve, f_in, t * PICKS + j - 3)
                            dve.scalar_tensor_tensor(junk[:, j % 4, :], ring[:, j % RING, 0:D], 1.0, xc[:, s, :],
                                                     ALU.mult, ALU.mult, accum_out=inner[:, h % 2, k:k + 1])\
                               .then_inc(f_in, 1)
                        dve.wait_ge(f_in, t * PICKS + (h + 1) * TOPK)
                        if not static(t) or t * HEADS + h >= 2:
                            dve.wait_ge(f_dg, (t * HEADS + h - 1) * TOPK)
                        dve.scalar_tensor_tensor(vals[:, h % 2, :], inner[:, h % 2, :], 0.0, prob[:, s, h, :],
                                                 ALU.max, ALU.mult).then_inc(f_val, 1)
                        if look and h < 4:
                            look_up_head(t + 1, 2 * h)
                            look_up_head(t + 1, 2 * h + 1)
                        if node and h < 7:
                            (node_sum, node_x, node_clamp, node_mish, node_y, node_x2, node_xf)[h](t + 2)
                        if look and h == 4:
                            finish(t + 1, 1 - s)
                    dve.wait_ge(f_xr, t + 1)
                    dve.wait_ge(f_pe, (t + 1) * PICKS)
                    dve.tensor_tensor(xr[:, s, :], banks[s][0:R, :], xr[:, s, :], ALU.add).then_inc(f_o, 1)
                run_tiles(dve, tile)

            @block.tensor
            def _(pe):
                def transposes(bank, rows):
                    for k in range(KC):
                        last = pe.transpose(bank[:, 128 * k:128 * k + R], rows[:, 128 * k:128 * (k + 1)],
                                            ident[0:R, 0:R])
                    return last

                def products(bank, cols, w):
                    for k in range(KC):
                        last = pe.matmul(bank[0:R, :], cols[:, k, 0:R], w[:, k, :], start=(k == 0), stop=(k == KC - 1))
                    return last

                def node_T(u):
                    pe.wait_ge(m_ag, u + 1)
                    need(pe, m_hT, u)
                    transposes(banks[2], AG).then_inc(m_T, 1)

                def node_w3(u):
                    pe.wait_ge(m_aT, u + 1)
                    need(pe, m_y1, u)
                    products(banks[3], aT, w3a).then_inc(m_3, 1)

                def node_T2(u):
                    pe.wait_ge(m_h, u + 1)
                    pe.wait_ge(m_aT, u + 1)
                    transposes(banks[2], MH).then_inc(m_T2, 1)

                def node_w4(u):
                    pe.wait_ge(m_hT, u + 1)
                    pe.wait_ge(m_x, u + 1)
                    products(banks[3], hT3, w4).then_inc(m_4, 1)

                def node_all(u):
                    for part in (node_T, node_w3, node_T2, node_w4):
                        part(u)

                def transposed(tq):
                    pe.wait_ge(m_xf, tq + 1)
                    need(pe, f_qs, tq * HEADS)
                    transposes(banks[4], xfn).then_inc(f_T, 1)

                def queries(tq, h):
                    q = tq * HEADS + h
                    pe.wait_ge(f_xT, tq + 1)
                    need(pe, f_qs, q - 1)
                    for k in range(KC):
                        last = pe.matmul(q_bank[h % 2][:, 0:R], wq[:, k, 128 * h:128 * (h + 1)], xqT[:, k, 0:R],
                                         start=(k == 0), stop=(k == KC - 1))
                    last.then_inc(f_q, 1)

                def scores(tq, h):
                    q = tq * HEADS + h
                    pe.wait_ge(f_qs, q + 1)
                    need(pe, f_top, q - 1)
                    for a in range(2):
                        half = slice(HALF * a, HALF * (a + 1))
                        if a:
                            pe.wait_ge(f_s, 2 * q + 1)
                        pe.matmul(s_bank[h % 2][0:R, NKEYS * a:NKEYS * (a + 1)], qh[half, h % 2, 0:R],
                                         keys[half, NKEYS * h:NKEYS * (h + 1)], start=True, stop=True).then_inc(f_s, 1)

                pe.wait_ge(c_wlate, 64)
                node_all(0)
                transposed(0)
                queries(0, 0)
                for h in range(HEADS):
                    if h + 1 < HEADS:
                        queries(0, h + 1)
                    scores(0, h)
                node_all(1)

                def tile(s, i, look, node):
                    t = 2 * i + s
                    for h in range(HEADS):
                        if look and h == 0:
                            transposed(t + 1)
                        if node and h == 1:
                            node_T(t + 2)
                        if look and h < 4:
                            for part in (queries, scores):
                                part(t + 1, 2 * h)
                                part(t + 1, 2 * h + 1)
                        if node and h == 1:
                            node_w3(t + 2)
                        if node and h == 4:
                            node_T2(t + 2)
                            node_w4(t + 2)
                        for k in range(TOPK):
                            j = h * TOPK + k
                            pe.wait_ge(f_dg, t * PICKS + j + 1)
                            if j == 0:
                                need(pe, f_o, t - 1)
                            pe.matmul(banks[s][0:R, :], dg[:, j % DSLOTS, 0:R], ring[:, j % RING, D:2 * D],
                                      start=(j == 0), stop=(j == PICKS - 1)).then_inc(f_pe, 1)
                run_tiles(pe, tile)


def kernel(**inputs):
    import numpy as np
    import concourse.bacc as bacc
    from concourse import mybir as mb
    from concourse.bass_utils import run_bass_kernel_spmd

    a = {k: np.asarray(v) for k, v in inputs.items()}
    rows = 125
    src, dst, ea = a["src"], a["dst"], a["edge_attr_64"]
    keys = a["L0_ffn_keys"]
    heads, halves, n_keys, width = keys.shape
    laid = {
        "x": a["x"],
        "src_cols": src.reshape(rows, -1),
        "dst_cols": dst.reshape(rows, -1),
        "dst_row": dst.reshape(rows, -1).T.reshape(1, -1),
        "ea_t": ea.reshape(rows, -1, ea.shape[1]).transpose(2, 1, 0).reshape(ea.shape[1], -1),
        **{n: a[f"L0_gnn_{n}"] for n in ("W1", "b1", "W2", "b2", "W3", "b3", "W4", "b4", "gamma", "beta")},
        "Wq": a["L0_ffn_Wq"],
        "bq_cols": a["L0_ffn_bq"].reshape(heads, -1).T,
        "keys_t": keys.transpose(1, 3, 0, 2).reshape(halves * width, heads * n_keys),
        "w_du": np.concatenate([a["L0_ffn_w_down"], a["L0_ffn_w_up"]], axis=1),
    }
    nc = bacc.Bacc("TRN2", target_bir_lowering=False, num_devices=1)
    arrays, args = {}, []
    for name, v in laid.items():
        v = np.ascontiguousarray(v)
        arrays[f"in_{name}"] = v
        args.append(nc.dram_tensor(f"in_{name}", v.shape, mb.dt.from_np(v.dtype), kind="ExternalInput").ap())
    out = nc.dram_tensor("out_0", a["x"].shape, mb.dt.float32, kind="ExternalOutput").ap()
    gnn_peer_kernel(nc, *args, out)
    r = run_bass_kernel_spmd(nc, [arrays], core_ids=[0])
    return r.results[0]["out_0"]
```

```python
import concourse.bass as bass
from concourse import mybir
from contextlib import ExitStack


def gnn_peer_kernel(nc, x, src_cols, dst_cols, dst_row, ea_t, W1, b1, W2, b2, W3, b3, W4, b4,
                    gamma, beta, Wq, bq_cols, keys_t, w_du, out):
    f32 = mybir.dt.float32
    i32, u32 = mybir.dt.int32, mybir.dt.uint32
    ALU = mybir.AluOpType
    ACT = mybir.ActivationFunctionType
    AX = mybir.AxisListType.X

    NODES, D = x.shape
    EC, EDGES = ea_t.shape
    R = src_cols.shape[0]
    NT = NODES // R
    ET = EDGES // R
    KC = D // 128
    HEADS, TOPK = 8, 8
    HALF = keys_t.shape[0] // 2
    NKEYS = keys_t.shape[1] // HEADS
    PICKS = HEADS * TOPK
    CPT = ET // NT
    EPS = 1e-5
    LN2 = 0.6931471805599453
    ACT_TABLES = "natural_log_exp_and_others"
    UMAX = 1e9
    WIDE = 33546
    DSLOTS = 8
    RING = 24
    assert NT * R == NODES and ET * R == EDGES and CPT * NT == ET and NT % 2 == 0

    ctx = ExitStack()
    with ctx:
        def sb(name, shape, dt=f32):
            return ctx.enter_context(nc.sbuf_tensor(name, shape, dt))

        def sem(name):
            return ctx.enter_context(nc.semaphore(name))

        def sems(name, n):
            return [sem(f"{name}{k}") for k in range(n)]

        def static(i):
            return isinstance(i, int)

        def need(eng, s, value):
            if not isinstance(value, int) or value > 0:
                eng.wait_ge(s, value)

        def wait_alone(eng, s, value):
            need(eng, s, value)
            if not isinstance(value, int):
                eng.sem_inc(passed, 1)

        P_d = nc.dram_tensor("P_d", (NODES, D), f32, kind="Internal").ap()
        Q_d = nc.dram_tensor("Q_d", (NODES, D), f32, kind="Internal").ap()
        xn_d = nc.dram_tensor("xn_d", (NODES, D), f32, kind="Internal").ap()
        agg_d = [nc.dram_tensor(f"agg{k}_d", (NODES + R, D), f32, kind="Internal").ap() for k in range(2)]

        ident = sb("ident", [128, 128])
        before = sb("before", [128, 128])
        srcc = sb("srcc", [R, ET], i32)
        dsti = sb("dsti", [R, ET], i32)
        dstf = sb("dstf", [R, ET])
        sidx = sb("sidx", [R, ET], i32)
        dummy = sb("dummy_row", [R, 1])
        ones = sb("ones", [R, 128])
        cnt = sb("cnt", [R, ET])
        cnts = sb("cnts", [R, 1])
        shared = sb("shared", [1, 1], i32)
        eps = sb("eps", [128, 1])
        ln2 = sb("ln2", [128, 1])
        b12 = sb("b12", [128, 2, D])
        b1b, b2b = b12[:, 0, :], b12[:, 1, :]
        b3b, b4b = sb("b3b", [128, D]), sb("b4b", [128, D])
        gab, beb = sb("gab", [128, D]), sb("beb", [128, D])
        bqc = sb("bqc", [128, HEADS])
        iota8 = sb("iota8", [R, TOPK])
        w1a = sb("w1a", [128, 2 * KC, D])
        w1c = sb("w1c", [EC, D])
        w2 = sb("w2", [128, KC, D])
        w3x = sb("w3x", [128, KC, D])
        wide = sb("wide", [128, WIDE])
        wq = sb("wq", [128, KC, HEADS * 128])
        keys = sb("keys", [128, HEADS * NKEYS])
        banks = [ctx.enter_context(nc.psum_tensor(f"bank{k}", [128, 512], f32)) for k in range(8)]
        w3a, w4 = w1a[:, 0:KC, :], w1a[:, KC:2 * KC, :]

        def carve(at, rows, *dims):
            n = 1
            for d in dims:
                n *= d
            v = wide[0:rows, at:at + n]
            if len(dims) == 2:
                v = v.rearrange("p (a b) -> p a b", a=dims[0])
            elif len(dims) == 3:
                v = v.rearrange("p (a b c) -> p a b c", a=dims[0], b=dims[1])
            return v, at + n

        c_in, c_w1, c_cst, c_cst2 = sem("c_in"), sem("c_w1"), sem("c_cst"), sem("c_cst2")
        passed = sem("passed")
        c_idx, c_wlate = sem("c_idx"), sem("c_wlate")
        n_x, n_row = sems("n_x", 2), sems("n_row", 2)
        n_stat, n_mv, n_lv, n_rs, n_xn = (sem(n) for n in ("n_stat", "n_mv", "n_lv", "n_rs", "n_xn"))
        n_T, n_xt, n_mm, n_ev, n_evp = (sem(n) for n in ("n_T", "n_xt", "n_mm", "n_ev", "n_evp"))
        n_dc, n_dup, n_dd, n_m, n_sx = (sem(n) for n in ("n_dc", "n_dup", "n_dd", "n_m", "n_sx"))
        n_cs, n_any, n_sh = sem("n_cs"), sem("n_any"), sem("n_sh")
        n_st, n_sto, n_zero = sems("n_st", 2), sems("n_sto", 2), sem("n_zero")

        at = 0
        xt, at = carve(at, R, 2, D)
        xn, at = carve(at, R, 2, D)
        xnT, at = carve(at, 128, 2, KC, 128)
        pq, at = carve(at, R, 2, 2, D)
        zero, at = carve(at, R, D)
        rows0, at = carve(at, 128, 2, CPT * R)
        rows0 = rows0.bitcast(i32)
        st, at = carve(at, R, 2, 6)
        mv, at = carve(at, R, 2, 2)
        lv, at = carve(at, R, 2, 2)
        dc, at = carve(at, R, CPT)
        dd, at = carve(at, R, CPT)
        mm, at = carve(at, R, CPT)
        hit, at = carve(at, R, 4, R)
        assert at <= WIDE

        def in_range(c, i, lo=0, hi=ET):
            return not static(i) or lo <= c < hi

        def rows_of(table, t):
            return table[bass.ds(t * R, R), :]

        with nc.Block() as block:
            @block.sync
            def _(sp):
                def load_x(c, i):
                    need(sp, n_xn, c + 2 * i - 1)
                    sp.dma_start(xt[:, c % 2, :], rows_of(x, c + 2 * i)).then_inc(n_x[c % 2], 16)

                def load_row(c, i):
                    need(sp, n_dup, (c + 2 * i - 1) * CPT)
                    sp.dma_start(rows0[:, c % 2, :],
                                 dst_row[0:1, bass.ds((c + 2 * i) * (CPT * R), CPT * R)]
                                 .to_broadcast([128, CPT * R])).then_inc(n_row[c % 2], 16)

                load_x(0, 0)
                for m in range(2):
                    sp.dma_start(w1a[:, m * KC:(m + 1) * KC, :],
                                 W1[m * D:(m + 1) * D, :].rearrange("(k p) n -> p k n", p=128)).then_inc(c_w1, 16)
                    if m == 0:
                        load_x(1, 0)
                for dst_, src_ in ((srcc, src_cols), (dsti, dst_cols)):
                    sp.dma_start(dst_[:, :], src_).then_inc(c_idx, 16)
                load_row(0, 0)
                load_row(1, 0)

                def step(c, i):
                    if not static(i):
                        load_x(c, i)
                        load_row(c, i)
                    t = c - 2
                    if t >= 0:
                        sp.wait_ge(n_ev, t + 2 * i + 1)
                        sp.wait_ge(n_evp, t + 2 * i + 1)
                        for k, table in enumerate((P_d, Q_d)):
                            sp.dma_start(rows_of(table, t + 2 * i), pq[:, t % 2, k, :]).then_inc(n_st[t % 2], 16)
                with sp.Fori(0, (NT - 2) // 2) as i:
                    step(2, i)
                    step(3, i)
                step(NT, 0)
                step(NT + 1, 0)
                for k in range(2):
                    sp.wait_ge(n_st[k], 32 * (NT // 2))

            @block.gpsimd
            def _(pool):
                pool.memset(ident[:, :], 0.0).then_inc(c_cst, 1)
                pool.memset(before[:, :], 1.0).then_inc(c_cst, 1)
                pool.wait_ge(c_cst, 2)
                pool.affine_select(out=ident[:, :], in_=ident[:, :], compare_op=ALU.not_equal, fill=1.0,
                                   base=0, pattern=[[-1, 128]], channel_multiplier=1).then_inc(c_cst, 1)
                pool.affine_select(out=before[:, :], in_=before[:, :], compare_op=ALU.is_gt, fill=0.0,
                                   base=0, pattern=[[-1, 128]], channel_multiplier=1).then_inc(c_cst, 1)
                pool.iota(dummy[:, :], [[0, 1]], base=NODES, channel_multiplier=1,
                          allow_small_or_imprecise_dtypes=True).then_inc(c_cst, 1)
                pool.iota(iota8[:, :], [[1, TOPK]], base=0, channel_multiplier=0,
                          allow_small_or_imprecise_dtypes=True).then_inc(c_cst, 1)
                pool.memset(eps[:, :], EPS).then_inc(c_cst, 1)
                pool.memset(ln2[:, :], LN2).then_inc(c_cst, 1)
                pool.memset(zero[:, :], 0.0).then_inc(c_cst, 1)
                pool.memset(ones[:, :], 1.0).then_inc(c_cst, 1)

            @block.scalar
            def _(act):
                act.preload_act_table_set(ACT_TABLES)
                row = lambda v: v.rearrange("(a n) -> a n", a=1).to_broadcast([128, D])
                act.wait_ge(c_cst, 10)

                act.dma_start(b1b, row(b1)).then_inc(c_in, 16)
                for a in agg_d:
                    act.dma_start(a[NODES:NODES + R, :], zero[:, :]).then_inc(n_zero, 16)

                def step(c, i):
                    if c < NT or not static(i):
                        s = c % 2
                        act.wait_ge(n_mv, c + 2 * i + 1)
                        act.activation(lv[:, s, 0:1], mv[:, s, 1:2], ACT.Ln, bias=eps[0:R, :]).then_inc(n_lv, 1)
                        act.wait_ge(n_lv, c + 2 * i + 1)
                        act.activation(lv[:, s, 1:2], lv[:, s, 0:1], ACT.Exp, scale=-0.5).then_inc(n_rs, 1)
                    t = c - 2
                    if t >= 0:
                        act.wait_ge(n_mm, t + 2 * i + 1)
                        need(act, n_st[t % 2], 32 * (t // 2 + i))
                        act.activation(pq[:, t % 2, 0, :], banks[2 + 2 * (t % 2)][0:R, :], ACT.Copy).then_inc(n_evp, 1)
                    if c < NT or not static(i):
                        act.wait_ge(n_T, c + 2 * i + 1)
                        need(act, n_mm, c + 2 * i - 1)
                        act.activation(xnT[:, c % 2, :, 0:R],
                                       banks[c % 2][:, :].rearrange("p (k r) -> p k r", k=KC)[:, :, 0:R],
                                       ACT.Copy).then_inc(n_xt, 1)
                        act.wait_ge(n_xn, c + 2 * i + 1)
                        act.dma_start(rows_of(xn_d, c + 2 * i), xn[:, c % 2, :]).then_inc(n_sto[c % 2], 16)
                        for a in agg_d:
                            act.dma_start(rows_of(a, c + 2 * i), zero[:, :]).then_inc(n_zero, 16)
                step(0, 0)
                step(1, 0)
                with act.Fori(0, (NT - 2) // 2) as i:
                    step(2, i)
                    step(3, i)
                step(NT, 0)
                act.dma_start(w1c[:, :], W1[2 * D:2 * D + EC, :]).then_inc(c_cst2, 16)
                act.dma_start(b2b, row(b2)).then_inc(c_cst2, 16)
                act.dma_start(w2[:, :, :], W2.rearrange("(k p) n -> p k n", p=128)).then_inc(c_cst2, 16)
                step(NT + 1, 0)
                act.wait_ge(n_zero, 16 * 2 * (NT + 1))
                act.wait_ge(n_sto[0], 16 * NT // 2)
                act.wait_ge(n_sto[1], 16 * NT // 2)

            @block.vector
            def _(dve):
                dve.wait_ge(c_cst, 10)

                def step(c, i):
                    n, s = c + 2 * i, c % 2
                    if c < NT or not static(i):
                        dve.wait_ge(n_x[s], 16 * (c // 2 + i + 1))
                        dve.bn_stats(st[:, s, :], xt[:, s, :]).then_inc(n_stat, 1)
                        wait_alone(dve, n_stat, n + 1)
                        dve.bn_aggr(mv[:, s, :], st[:, s, :]).then_inc(n_mv, 1)
                    t = c - 2
                    if t >= 0:
                        if t == 0:
                            dve.wait_ge(c_in, 16)
                        dve.wait_ge(n_mm, t + 2 * i + 1)
                        need(dve, n_st[t % 2], 32 * (t // 2 + i))
                        dve.tensor_tensor(pq[:, t % 2, 1, :], banks[3 + 2 * (t % 2)][0:R, :], b1b[0:R, :],
                                          ALU.add).then_inc(n_ev, 1)
                    if c < NT or not static(i):
                        dve.wait_ge(n_rs, n + 1)
                        need(dve, n_T, n - 1)
                        need(dve, n_sto[s], 16 * (c // 2 + i))
                        dve.tensor_scalar(xn[:, s, :], xt[:, s, :], mv[:, s, 0:1], lv[:, s, 1:2],
                                          ALU.subtract, ALU.mult).then_inc(n_xn, 1)
                    if c == 1:
                        dve.wait_ge(c_idx, 32)
                        dve.tensor_copy(dstf[:, :], dsti[:, :]).then_inc(n_sx, 1)
                        dve.wait_ge(n_sx, 1)
                    if in_range(c - 1, i, 0, NT):
                        m, t = n - 1, c - 1
                        dve.wait_ge(n_sx, m + 1)
                        dve.tensor_copy(dc[:, :], dstf[:, bass.ds(m * CPT, CPT)]).then_inc(n_dc, 1)
                        dve.wait_ge(n_dc, m + 1)
                        dve.wait_ge(n_row[t % 2], 16 * (t // 2 + i + 1))
                        for k in range(CPT):
                            need(dve, n_dup, m * CPT + k - 3)
                            dve.scalar_tensor_tensor(
                                hit[:, k % 4, :], rows0[0:R, t % 2, k * R:(k + 1) * R], dc[:, k:k + 1],
                                before[0:R, 0:R], ALU.is_equal, ALU.mult,
                                accum_out=cnt[:, bass.ds(m * CPT + k, 1)]).then_inc(n_dup, 1)
                        dve.tensor_scalar(dd[:, :], dc[:, :], -1.0, dummy[:, 0:1], ALU.mult, ALU.add).then_inc(n_dd, 1)
                        dve.wait_ge(n_dup, (m + 1) * CPT)
                        dve.wait_ge(n_dd, m + 1)
                        dve.scalar_tensor_tensor(mm[:, :], cnt[:, bass.ds(m * CPT, CPT)], 0.0, dd[:, :],
                                                 ALU.is_gt, ALU.mult).then_inc(n_m, 1)
                        dve.wait_ge(n_m, m + 1)
                        dve.tensor_tensor(sidx[:, bass.ds(m * CPT, CPT)], mm[:, :], dc[:, :], ALU.add).then_inc(n_sx, 1)
                step(0, 0)
                step(1, 0)
                with dve.Fori(0, (NT - 2) // 2) as i:
                    step(2, i)
                    step(3, i)
                step(NT, 0)
                dve.wait_ge(n_dup, ET)
                dve.tensor_reduce(cnts[:, :], cnt[:, :], AX, ALU.add).then_inc(n_cs, 1)
                step(NT + 1, 0)
                dve.wait_ge(n_any, 1)
                dve.tensor_scalar(shared[:, :], banks[0][0:1, 0:1], 1.0, None, ALU.min).then_inc(n_sh, 1)
                dve.wait_ge(n_sh, 1)

            @block.tensor
            def _(pe):
                pe.wait_ge(c_cst, 10)

                def step(c, i):
                    if c < NT or not static(i):
                        n = c + 2 * i
                        pe.wait_ge(n_xn, n + 1)
                        need(pe, n_xt, n - 1)
                        for k in range(KC):
                            last = pe.transpose(banks[c % 2][:, 128 * k:128 * k + R],
                                                xn[:, c % 2, 128 * k:128 * (k + 1)], ident[0:R, 0:R])
                        last.then_inc(n_T, 1)
                    t = c - 1
                    if t >= 0:
                        pe.wait_ge(n_xt, t + 2 * i + 1)
                        need(pe, n_ev, t + 2 * i - 1)
                        need(pe, n_evp, t + 2 * i - 1)
                        for m in range(2):
                            for k in range(KC):
                                last = pe.matmul(banks[2 + 2 * (t % 2) + m][0:R, :], xnT[:, t % 2, k, 0:R],
                                                 w1a[:, m * KC + k, :],
                                                 start=(k == 0), stop=(k == KC - 1))
                        last.then_inc(n_mm, 1)
                step(0, 0)
                pe.wait_ge(c_w1, 32)
                step(1, 0)
                with pe.Fori(0, (NT - 2) // 2) as i:
                    step(2, i)
                    step(3, i)
                step(NT, 0)
                pe.wait_ge(n_cs, 1)
                pe.wait_ge(n_xt, NT)
                pe.matmul(banks[0][:, 0:1], ones[:, :], cnts[:, :], start=True, stop=True).then_inc(n_any, 1)

        LAG = 4
        PASSES = ET + LAG
        FIRST, LAST = 12, ET - 2
        assert (LAST - FIRST) % 4 == 0
        e_ea, e_row, e_gat = sems("e_ea", 2), sems("e_row", 2), sems("e_gat", 4)
        e_E, e_T, e_W2, e_S = (sem(n) for n in ("e_E", "e_T", "e_W2", "e_S"))
        e_a1, e_pre, e_x2, e_sel = (sem(n) for n in ("e_a1", "e_pre", "e_x2", "e_sel"))
        e_u, e_c, e_v, e_ln, e_r, e_h = (sem(n) for n in ("e_u", "e_c", "e_v", "e_ln", "e_r", "e_h"))
        e_hT, e_ms, e_ix, e_sc, e_sci = sem("e_hT"), sem("e_ms"), sem("e_ix"), sems("e_sc", 2), sem("e_sci")
        e_dcol = sem("e_dcol")
        at = 0
        G, at = carve(at, R, 4, 2, D)
        X, at = carve(at, R, 4, 2 * D)
        U, at = carve(at, R, 2, 2 * D)
        V, at = carve(at, R, 2, 2 * D)
        H, at = carve(at, R, 4, 2 * D)
        hT, at = carve(at, 128, 2, KC, 128)
        sel, at = carve(at, R, 2, R)
        ea, at = carve(at, EC, 2, 2 * R)
        rowb, at = carve(at, 128, 2, 2 * R)
        rowb = rowb.bitcast(i32)
        gix, at = carve(at, R, 4, 2)
        gix = gix.bitcast(i32)
        six, at = carve(at, R, 4, 1)
        six = six.bitcast(i32)
        dcol, at = carve(at, R, 2, 1)
        msum = H[:, 2:4].rearrange("p s (a n) -> p (s a) n", a=2)
        assert at <= WIDE
        Eb, Tb, Wb, Sb = banks[0:2], banks[2:4], banks[4:6], banks[6:8]

        def span(c, i):
            if not static(i):
                return 0, 2 * D
            return (0 if c < ET else D), (2 * D if c >= LAG else D)

        def run(eng, step, first=0, last=ET + 9):
            for n in range(first, FIRST):
                step(n, 0)
            with eng.Fori(0, (LAST - FIRST) // 4) as i:
                for c in range(FIRST, FIRST + 4):
                    step(c, i)
            for n in range(LAST, last):
                step(n, 0)

        def edges(plain):
            HS = 4 if plain else 2
            with nc.Block() as block:
                @block.sync
                def _(sp):
                    def load(g, j):
                        if g < ET // 2:
                            need(sp, e_E, 2 * (g + 2 * j) - 2)
                            sp.dma_start(ea[:, g % 2, :], ea_t[:, bass.ds((g + 2 * j) * (2 * R), 2 * R)])\
                              .then_inc(e_ea[g % 2], 16)
                        q = -1 if plain else g - 3
                        if q >= 0:
                            need(sp, e_sel, 2 * (q + 2 * j) - 2)
                            sp.dma_start(rowb[:, q % 2, :],
                                         dst_row[0:1, bass.ds((q + 2 * j) * (2 * R), 2 * R)].to_broadcast([128, 2 * R]))\
                              .then_inc(e_row[q % 2], 16)
                    for g in range(5):
                        load(g, 0)
                    for dst_, src_ in ((w3x[:, :, :], W3[0:D, :]), (w3a, W3[D:2 * D, :]), (w4, W4), (wq[:, :, :], Wq)):
                        sp.dma_start(dst_, src_.rearrange("(k p) n -> p k n", p=128)).then_inc(c_wlate, 16)
                    sp.dma_start(keys[:, :], keys_t).then_inc(c_wlate, 16)
                    sp.dma_start(bqc[:, :], bq_cols).then_inc(c_wlate, 16)
                    for dst_, v in ((b3b, b3), (b4b, b4), (gab, gamma), (beb, beta)):
                        sp.dma_start(dst_[:, :], v.rearrange("(a n) -> a n", a=1).to_broadcast([128, D]))\
                          .then_inc(c_wlate, 16)
                    with sp.Fori(0, (ET // 2 - 5) // 2) as j:
                        load(5, j)
                        load(6, j)
                    for g in range(ET // 2, ET // 2 + 3):
                        load(g, 0)

                @block.gpsimd
                def _(pool):
                    def step(c, i):
                        if in_range(c + 2, i):
                            t, k = c + 2, (c + 2) % 4
                            need(pool, e_gat[k], 32 * (t // 4 + i))
                            wait_alone(pool, e_pre, t + 4 * i - 3)
                            pool.tensor_copy(gix[:, k, 0:1], srcc[:, bass.ds(t + 4 * i, 1)]).then_inc(e_ix, 1)
                            pool.tensor_copy(gix[:, k, 1:2], dsti[:, bass.ds(t + 4 * i, 1)]).then_inc(e_ix, 1)
                            wait_alone(pool, e_ix, 2 * (t + 4 * i) + 2)
                            for m, table in enumerate((P_d, Q_d)):
                                pool.indirect_dma_start(
                                    out=G[:, k, m, :], out_offset=None, in_=table,
                                    in_offset=bass.IndirectOffsetOnAxis(ap=gix[:, k, m:m + 1], axis=0),
                                    bounds_check=NODES - 1, oob_is_err=True).then_inc(e_gat[k], 16)
                        back = 8 if plain else 9
                        if in_range(c - back, i):
                            t, k = c - back, (c - back) % 4
                            wait_alone(pool, e_sc[t % 2], 16 * (t // 2 + 2 * i))
                            pool.tensor_copy(six[:, k, :], sidx[:, bass.ds(t + 4 * i, 1)]).then_inc(e_sci, 1)
                            pool.wait_ge(e_sci, t + 4 * i + 1)
                            if plain:
                                wait_alone(pool, e_h, t + 4 * i + LAG + 1)
                            else:
                                wait_alone(pool, e_ms, t + 4 * i + 1)
                            pool.indirect_dma_start(
                                out=agg_d[t % 2], out_offset=bass.IndirectOffsetOnAxis(ap=six[:, k, :], axis=0),
                                in_=H[:, k, D:2 * D] if plain else msum[:, k, :], in_offset=None,
                                bounds_check=NODES + R - 1, oob_is_err=True, compute_op=ALU.add)\
                                .then_inc(e_sc[t % 2], 16)
                    run(pool, step, first=-2)
                    for k in range(2):
                        pool.wait_ge(e_sc[k], 16 * (ET // 2))

                @block.scalar
                def _(act):
                    act.preload_act_table_set(ACT_TABLES)
                    def step(c, i):
                        n = c + 4 * i
                        if in_range(c - 3, i, 0, PASSES):
                            p = c - 3
                            lo, hi = span(p, i)
                            v = V[:, p % 2, lo:hi]
                            act.wait_ge(e_v, n - 2)
                            act.activation(v, v, ACT.Ln, bias=1.0).then_inc(e_ln, 1)
                        if in_range(c - 2, i, 0, PASSES):
                            p = c - 2
                            lo, hi = span(p, i)
                            if in_range(p, i):
                                act.wait_ge(e_pre, n - 1)
                            if in_range(p - LAG, i):
                                act.wait_ge(e_x2, n - 1 - LAG)
                            act.activation(U[:, p % 2, lo:hi], X[:, p % 4, lo:hi], ACT.Exp).then_inc(e_u, 1)
                        if in_range(c - 3, i, 0, PASSES):
                            act.wait_ge(e_ln, n - 2)
                            act.activation(v, v, ACT.Exp, bias=ln2[0:R, :], scale=-1.0).then_inc(e_r, 1)
                        if in_range(c - 2, i, 0, PASSES):
                            p = c - 2
                            lo, hi = span(p, i)
                            act.wait_ge(e_c, n - 1)
                            need(act, e_h, n - 3)
                            act.activation(V[:, p % 2, lo:hi], U[:, p % 2, lo:hi], ACT.Square).then_inc(e_v, 1)
                        if in_range(c - 4, i):
                            t = c - 4
                            act.wait_ge(e_T, n - 3)
                            need(act, e_W2, n - 5)
                            act.activation(hT[:, t % 2, :, 0:R],
                                           Tb[t % 2][:, :].rearrange("p (k r) -> p k r", k=KC)[:, :, 0:R],
                                           ACT.Copy).then_inc(e_hT, 1)
                        if not plain and in_range(c - 8, i):
                            t = c - 8
                            act.wait_ge(e_S, n - 7)
                            need(act, e_sc[t % 2], 16 * ((t - 4) // 2 + 2 * i + 1))
                            act.activation(msum[:, t % 4, :], Sb[t % 2][0:R, :], ACT.Copy).then_inc(e_ms, 1)
                    run(act, step)

                @block.vector
                def _(dve):
                    def step(c, i):
                        n = c + 4 * i
                        if in_range(c - 6, i):
                            t = c - 6
                            dve.wait_ge(e_W2, n - 5)
                            dve.tensor_tensor(X[:, (t + LAG) % 4, D:2 * D], Wb[t % 2][0:R, :], b2b[0:R, :],
                                              ALU.add).then_inc(e_x2, 1)
                        if in_range(c - 1, i):
                            t = c - 1
                            k = t % 4
                            dve.wait_ge(e_E, n)
                            dve.wait_ge(e_gat[k], 32 * (t // 4 + i + 1))
                            dve.tensor_tensor(X[:, k, 0:D], Eb[t % 2][0:R, :], G[:, k, 0, :], ALU.add).then_inc(e_a1, 1)
                            dve.wait_ge(e_a1, n)
                            dve.tensor_tensor(X[:, k, 0:D], X[:, k, 0:D], G[:, k, 1, :], ALU.add).then_inc(e_pre, 1)
                        if not plain and in_range(c - 7, i):
                            t = c - 7
                            dve.wait_ge(e_row[(t // 2) % 2], 16 * (t // 4 + i + 1))
                            dve.tensor_copy(dcol[:, t % 2, :], dstf[:, bass.ds(t + 4 * i, 1)]).then_inc(e_dcol, 1)
                            dve.wait_ge(e_dcol, n - 6)
                            need(dve, e_S, n - 8)
                            dve.tensor_scalar(sel[:, t % 2, :], rowb[0:R, (t // 2) % 2, (t % 2) * R:(t % 2 + 1) * R],
                                              dcol[:, t % 2, :], None, ALU.is_equal).then_inc(e_sel, 1)
                        if in_range(c - 2, i, 0, PASSES):
                            p = c - 2
                            lo, hi = span(p, i)
                            u = U[:, p % 2, lo:hi]
                            dve.wait_ge(e_u, n - 1)
                            dve.tensor_scalar(u, u, UMAX, 1.0, ALU.min, ALU.add).then_inc(e_c, 1)
                        if in_range(c - 3, i, 0, PASSES):
                            p = c - 3
                            lo, hi = span(p, i)
                            dve.wait_ge(e_r, n - 2)
                            need(dve, e_T, min(p - HS + 1, ET) if static(i) else n - 2 - HS)
                            if not plain:
                                need(dve, e_S, n - 2 - HS - LAG)
                            elif p >= HS + LAG:
                                dve.wait_ge(e_sc[p % 2], 16 * ((p - HS - LAG) // 2 + 2 * i + 1))
                            dve.scalar_tensor_tensor(H[:, p % HS, lo:hi], V[:, p % 2, lo:hi], 1.0, X[:, p % 4, lo:hi],
                                                     ALU.subtract, ALU.mult, reverse0=True).then_inc(e_h, 1)
                    dve.wait_ge(c_cst2, 48)
                    run(dve, step)

                @block.tensor
                def _(pe):
                    def step(c, i):
                        n = c + 4 * i
                        if in_range(c - 4, i):
                            t = c - 4
                            pe.wait_ge(e_h, n - 3)
                            need(pe, e_hT, n - 5)
                            for k in range(KC):
                                last = pe.transpose(Tb[t % 2][:, 128 * k:128 * k + R],
                                                    H[:, t % HS, 128 * k:128 * (k + 1)], ident[0:R, 0:R])
                            last.then_inc(e_T, 1)
                        if not plain and in_range(c - 8, i):
                            t = c - 8
                            pe.wait_ge(e_h, n - 3)
                            pe.wait_ge(e_sel, n - 7)
                            need(pe, e_ms, n - 9)
                            pe.matmul(Sb[t % 2][0:R, :], sel[:, t % 2, :], H[:, t % HS, D:2 * D],
                                      start=True, stop=True).then_inc(e_S, 1)
                        if in_range(c, i):
                            g = (c // 2) % 2
                            pe.wait_ge(e_ea[g], 16 * (c // 4 + i + 1))
                            need(pe, e_pre, n - 1)
                            pe.matmul(Eb[c % 2][0:R, :], ea[:, g, (c % 2) * R:(c % 2 + 1) * R], w1c[:, :],
                                      start=True, stop=True).then_inc(e_E, 1)
                        if in_range(c - 5, i):
                            t = c - 5
                            pe.wait_ge(e_hT, n - 4)
                            need(pe, e_x2, n - 6)
                            for k in range(KC):
                                last = pe.matmul(Wb[t % 2][0:R, :], hT[:, t % 2, k, 0:R], w2[:, k, :],
                                                 start=(k == 0), stop=(k == KC - 1))
                            last.then_inc(e_W2, 1)
                    pe.wait_ge(c_cst2, 48)
                    run(pe, step)

        two_of_a_node = nc.values_load(shared[:, :], min_val=0, max_val=1)
        with nc.If(two_of_a_node == 0):
            edges(True)
        with nc.Else():
            edges(False)

        m_in, m_in2 = sem("m_in"), sem("m_in2")
        m_Tx, m_xT, m_ag, m_T, m_aT, m_3, m_x = (sem(n) for n in ("m_Tx", "m_xT", "m_ag", "m_T", "m_aT", "m_3", "m_x"))
        m_u, m_c, m_v, m_ln, m_r, m_h = (sem(n) for n in ("m_u", "m_c", "m_v", "m_ln", "m_r", "m_h"))
        m_T2, m_hT, m_4, m_y1, m_y = (sem(n) for n in ("m_T2", "m_hT", "m_4", "m_y1", "m_y"))
        m_s, m_mv, m_lv, m_rs, m_ch, m_xf = (sem(n) for n in ("m_s", "m_mv", "m_lv", "m_rs", "m_ch", "m_xf"))
        f_w, f_out = sems("f_w", RING), sems("f_out", 2)
        f_T, f_xT, f_q, f_qs, f_s = (sem(n) for n in ("f_T", "f_xT", "f_q", "f_qs", "f_s"))
        f_m, f_top, f_fin, f_e, f_idx = (sem(n) for n in ("f_m", "f_top", "f_fin", "f_e", "f_idx"))
        f_in, f_val, f_dg, f_pe, f_o = (sem(n) for n in ("f_in", "f_val", "f_dg", "f_pe", "f_o"))
        f_m2, f_rc, f_prob, f_xc, f_xr = (sem(n) for n in ("f_m2", "f_rc", "f_prob", "f_xc", "f_xr"))
        at = 0
        ring, at = carve(at, R, RING - 1, 2 * D)
        ring = [ring[:, k, :] for k in range(RING - 1)] + [b12[0:R, :, :].rearrange("p a n -> p (a n)")]
        A, at = carve(at, R, 2, D)
        MU = A[:, 1, :]
        XN, at = carve(at, R, 2, D)
        aT, at = carve(at, 128, KC, 128)
        xnT3, at = carve(at, 128, KC, 128)
        MX, at = carve(at, R, D)
        x2n, at = carve(at, R, D)
        xfn, at = carve(at, R, D)
        xqT, at = carve(at, 128, KC, 128)
        qh, at = carve(at, 128, 2, 128)
        xc, at = carve(at, R, 2, D)
        xr, at = carve(at, R, 2, D)
        sty, at = carve(at, R, 6)
        mvy, at = carve(at, R, 2)
        lvy, at = carve(at, R, 2)
        junk, at = carve(at, R, 2, D)
        dg, at = carve(at, R, DSLOTS, 128)
        eq, at = carve(at, R, D)
        assert at <= WIDE
        spare2 = w2[0:R, :, :].rearrange("p k n -> p (k n)")
        at2 = 0

        def small(n, dt=f32):
            nonlocal at2
            v = spare2[:, at2:at2 + n]
            at2 += n
            return v if dt is f32 else v.bitcast(dt)

        top = small(2 * PICKS).rearrange("p (h a k) -> p h a k", h=HEADS, a=2)
        topi = small(2 * PICKS, u32).rearrange("p (h a k) -> p h a k", h=HEADS, a=2)
        topf = small(2 * PICKS).rearrange("p (h a k) -> p h a k", h=HEADS, a=2)
        best = small(PICKS).rearrange("p (h k) -> p h k", h=HEADS)
        pos = small(PICKS, u32).rearrange("p (h k) -> p h k", h=HEADS)
        posi = small(PICKS, u32).rearrange("p (h k) -> p h k", h=HEADS)
        posj = small(PICKS, u32).rearrange("p (h k) -> p h k", h=HEADS)
        hi_f = small(PICKS).rearrange("p (h k) -> p h k", h=HEADS)
        lo_f = small(PICKS).rearrange("p (h k) -> p h k", h=HEADS)
        ex = small(PICKS).rearrange("p (h k) -> p h k", h=HEADS)
        es = small(HEADS)
        er = small(HEADS)
        prob = small(2 * PICKS).rearrange("p (s h k) -> p s h k", s=2, h=HEADS)
        idx = small(2 * PICKS, i32).rearrange("p (s j) -> p s j", s=2)
        inner = small(2 * TOPK).rearrange("p (s k) -> p s k", s=2)
        vals = small(2 * TOPK).rearrange("p (s k) -> p s k", s=2)
        comb = small(D)
        FIN = 11
        q_bank = (banks[7], banks[4])
        s_bank = banks[5:7]
        by_chunk = lambda bank: bank[:, :].rearrange("p (k r) -> p k r", k=KC)[:, :, 0:R]

        def slot_uses(k):
            return (PICKS - k + RING - 1) // RING

        def before_in_slot(j):
            return j - RING if j >= RING else j + RING * (slot_uses(j) - 1) - PICKS

        def run_tiles(eng, tile):
            tile(0, 0, True, True)
            tile(1, 0, True, True)
            with eng.Fori(1, NT // 2 - 1) as i:
                tile(0, i, True, True)
                tile(1, i, True, True)
            tile(0, NT // 2 - 1, True, False)
            tile(1, NT // 2 - 1, False, False)

        with nc.Block() as block:
            @block.sync
            def _(sp):
                def load(u):
                    need(sp, m_ch, 4 * u)
                    for k, table in enumerate((xn_d, x)):
                        sp.dma_start(XN[:, k, :], rows_of(table, u)).then_inc(m_in2, 16)
                    need(sp, m_h, u)
                    for k, table in enumerate(agg_d):
                        sp.dma_start(A[:, k, :], rows_of(table, u)).then_inc(m_in, 16)

                def store(t, s):
                    sp.wait_ge(f_o, t + 1)
                    sp.dma_start(rows_of(out, t), xr[:, s, :]).then_inc(f_out[s], 16)
                load(0)
                load(1)

                def tile(s, i, look, node):
                    t = 2 * i + s
                    if node:
                        load(t + 2)
                    if not static(t) or t > 0:
                        store(t - 1, 1 - s)
                run_tiles(sp, tile)
                store(NT - 1, 1)
                for s in range(2):
                    sp.wait_ge(f_out[s], 16 * (NT // 2))

            @block.gpsimd
            def _(pool):
                def tile(s, i, look, node):
                    t = 2 * i + s
                    wait_alone(pool, f_idx, t + 1)
                    for j in range(PICKS):
                        k = j % RING
                        if not static(t) or t * PICKS + j >= RING:
                            wait_alone(pool, f_pe, t * PICKS + before_in_slot(j) + 1)
                        pool.indirect_dma_start(
                            out=ring[k], out_offset=None, in_=w_du,
                            in_offset=bass.IndirectOffsetOnAxis(ap=idx[:, s, j:j + 1], axis=0),
                            bounds_check=NKEYS * NKEYS - 1, oob_is_err=True).then_inc(f_w[k], 16)
                run_tiles(pool, tile)

            @block.scalar
            def _(act):
                act.preload_act_table_set(ACT_TABLES)
                act.wait_ge(c_wlate, 160)

                def node_xn(u):
                    act.wait_ge(m_Tx, u + 1)
                    need(act, m_3, u)
                    act.activation(xnT3[:, :, 0:R], by_chunk(banks[3]), ACT.Copy).then_inc(m_xT, 1)

                def node_agg(u):
                    act.wait_ge(m_T, u + 1)
                    need(act, m_4, u)
                    act.activation(aT[:, :, 0:R], by_chunk(banks[2]), ACT.Copy).then_inc(m_aT, 1)

                def node_exp(u):
                    act.wait_ge(m_x, u + 1)
                    act.activation(MU, MX, ACT.Exp).then_inc(m_u, 1)

                def node_log(u):
                    act.wait_ge(m_c, u + 1)
                    act.activation(MU, MU, ACT.Square).then_inc(m_v, 1)
                    act.wait_ge(m_v, u + 1)
                    act.activation(MU, MU, ACT.Ln, bias=1.0).then_inc(m_ln, 1)
                    act.wait_ge(m_ln, u + 1)
                    act.activation(MU, MU, ACT.Exp, bias=ln2[0:R, :], scale=-1.0).then_inc(m_r, 1)

                def node_h(u):
                    act.wait_ge(m_T2, u + 1)
                    act.wait_ge(m_3, u + 1)
                    act.activation(aT[:, :, 0:R], by_chunk(banks[2]), ACT.Copy).then_inc(m_hT, 1)

                def node_norm(u, m):
                    act.wait_ge(m_mv, 2 * u + m + 1)
                    act.activation(lvy[:, 0:1], mvy[:, 1:2], ACT.Ln, bias=eps[0:R, :]).then_inc(m_lv, 1)
                    act.wait_ge(m_lv, 2 * u + m + 1)
                    act.activation(lvy[:, 1:2], lvy[:, 0:1], ACT.Exp, scale=-0.5).then_inc(m_rs, 1)

                def look_up_head(tq, h):
                    q = tq * HEADS + h
                    act.wait_ge(f_q, q + 1)
                    need(act, f_s, 2 * (q - 1))
                    act.activation(qh[:, h % 2, 0:R], q_bank[h % 2][:, 0:R], ACT.Identity,
                                   bias=bqc[:, h:h + 1]).then_inc(f_qs, 1)

                def transposed(tq):
                    act.wait_ge(f_T, tq + 1)
                    act.activation(xqT[:, :, 0:R], by_chunk(banks[4]), ACT.Copy).then_inc(f_xT, 1)

                def keep_xf(tq, s):
                    act.wait_ge(m_xf, tq + 1)
                    need(act, f_in, (tq - 1) * PICKS)
                    act.activation(xc[:, s, :], xfn, ACT.Copy).then_inc(f_xc, 1)

                def keep_x2(tq, s, stored):
                    need(act, f_out[s], 16 * stored)
                    act.activation(xr[:, s, :], x2n, ACT.Copy).then_inc(f_xr, 1)

                def exps(tq):
                    act.wait_ge(f_fin, tq * FIN + 2)
                    act.activation(ex, ex, ACT.Exp).then_inc(f_e, 1)

                def node_first(u):
                    node_xn(u)
                    node_agg(u)

                def node_rest(u):
                    node_exp(u)
                    node_log(u)
                    node_h(u)
                    node_norm(u, 0)
                    node_norm(u, 1)

                node_first(0)
                node_rest(0)
                transposed(0)
                for h in range(HEADS):
                    look_up_head(0, h)
                    if h == 2:
                        keep_xf(0, 0)
                    if h == 4:
                        keep_x2(0, 0, 0)
                node_first(1)
                exps(0)
                node_rest(1)

                def tile(s, i, look, node):
                    t = 2 * i + s
                    for h in range(1, HEADS + 1):
                        if look and h == 1:
                            transposed(t + 1)
                        if node and h == 1:
                            node_first(t + 2)
                        if look and 1 <= h <= 4:
                            look_up_head(t + 1, 2 * h - 2)
                            look_up_head(t + 1, 2 * h - 1)
                        if look and h == 2:
                            keep_xf(t + 1, 1 - s)
                        if look and h == 4:
                            keep_x2(t + 1, 1 - s, i + s)
                        if node:
                            if h == 2:
                                node_exp(t + 2)
                            if h == 3:
                                node_log(t + 2)
                            if h == 4:
                                node_h(t + 2)
                            if h in (6, 7):
                                node_norm(t + 2, h - 6)
                        act.wait_ge(f_val, t * HEADS + h)
                        for k in range(TOPK):
                            j = (h - 1) * TOPK + k
                            if not static(t) or t * PICKS + j >= DSLOTS:
                                act.wait_ge(f_pe, t * PICKS + j - DSLOTS + 1)
                            act.activation(dg[:, j % DSLOTS, 0:R], ident[0:R, 0:R], ACT.Copy,
                                           scale=vals[:, (h - 1) % 2, k:k + 1]).then_inc(f_dg, 1)
                        if look and h == 6:
                            exps(t + 1)
                run_tiles(act, tile)

            @block.vector
            def _(dve):
                def node_sum(u):
                    dve.wait_ge(m_in, 32 * (u + 1))
                    dve.tensor_tensor(A[:, 0, :], A[:, 0, :], A[:, 1, :], ALU.add).then_inc(m_ag, 1)

                def node_x(u):
                    dve.wait_ge(m_3, u + 1)
                    need(dve, m_T2, u)
                    dve.tensor_tensor(MX, banks[3][0:R, :], b3b[0:R, :], ALU.add).then_inc(m_x, 1)

                def node_clamp(u):
                    dve.wait_ge(m_u, u + 1)
                    dve.tensor_scalar(MU, MU, UMAX, 1.0, ALU.min, ALU.add).then_inc(m_c, 1)

                def node_mish(u):
                    dve.wait_ge(m_r, u + 1)
                    dve.scalar_tensor_tensor(MX, MU, 1.0, MX, ALU.subtract, ALU.mult, reverse0=True).then_inc(m_h, 1)

                def node_y(u):
                    dve.wait_ge(m_in2, 32 * (u + 1))
                    dve.wait_ge(m_4, u + 1)
                    need(dve, f_xr, u)
                    dve.tensor_tensor(x2n, banks[3][0:R, :], XN[:, 0, :], ALU.add).then_inc(m_y1, 1)
                    dve.wait_ge(m_y1, u + 1)
                    dve.tensor_tensor(x2n, x2n, b4b[0:R, :], ALU.add).then_inc(m_y, 1)
                    dve.wait_ge(m_y, u + 1)
                    dve.bn_stats(sty, x2n).then_inc(m_s, 1)
                    wait_alone(dve, m_s, 2 * u + 1)
                    dve.bn_aggr(mvy, sty).then_inc(m_mv, 1)

                def node_x2(u):
                    dve.wait_ge(m_rs, 2 * u + 1)
                    dve.tensor_scalar(x2n, x2n, mvy[:, 0:1], lvy[:, 1:2], ALU.subtract, ALU.mult).then_inc(m_ch, 1)
                    for k, other in enumerate((gab[0:R, :], beb[0:R, :], XN[:, 1, :])):
                        dve.wait_ge(m_ch, 4 * u + 1 + k)
                        dve.tensor_tensor(x2n, x2n, other, ALU.add if k else ALU.mult).then_inc(m_ch, 1)
                    dve.wait_ge(m_ch, 4 * u + 4)
                    dve.bn_stats(sty, x2n).then_inc(m_s, 1)
                    wait_alone(dve, m_s, 2 * u + 2)
                    dve.bn_aggr(mvy, sty).then_inc(m_mv, 1)

                def node_xf(u):
                    dve.wait_ge(m_rs, 2 * u + 2)
                    need(dve, f_T, u)
                    need(dve, f_xc, u)
                    dve.tensor_scalar(xfn, x2n, mvy[:, 0:1], lvy[:, 1:2], ALU.subtract, ALU.mult).then_inc(m_xf, 1)

                def node_rest(u):
                    for part in (node_x, node_clamp, node_mish, node_y, node_x2, node_xf):
                        part(u)

                def look_up_head(tq, h):
                    q = tq * HEADS + h
                    wait_alone(dve, f_s, 2 * q + 2)
                    for a in range(2):
                        sc = s_bank[h % 2][0:R, NKEYS * a:NKEYS * (a + 1)]
                        dve.max(out=top[:, h, a, :], in_=sc).then_inc(f_m, 1)
                    for a in range(2):
                        sc = s_bank[h % 2][0:R, NKEYS * a:NKEYS * (a + 1)]
                        wait_alone(dve, f_m, 2 * q + a + 1)
                        last = dve.max_index(topi[:, h, a, :], top[:, h, a, :], sc)
                    last.then_inc(f_top, 1)

                H3 = [R, HEADS, TOPK, TOPK]
                comb4 = comb.rearrange("p (h i j) -> p h i j", h=HEADS, i=TOPK)
                eq4 = eq.rearrange("p (h i j) -> p h i j", h=HEADS, i=TOPK)

                def finish(tq, s):
                    n = [0]

                    def link(ins):
                        n[0] += 1
                        ins.then_inc(f_fin, 1)
                        wait_alone(dve, f_fin, tq * FIN + n[0])
                    dve.wait_ge(f_top, tq * HEADS + HEADS)
                    dve.tensor_copy(topf, topi)
                    link(dve.tensor_tensor(comb4, top[:, :, 0, :].unsqueeze(3).to_broadcast(H3),
                                           top[:, :, 1, :].unsqueeze(2).to_broadcast(H3), ALU.add))
                    for h in range(HEADS):
                        last = dve.max(out=best[:, h, :], in_=comb[:, 64 * h:64 * (h + 1)])
                    last.then_inc(f_m2, 1)
                    wait_alone(dve, f_m2, tq + 1)
                    link(dve.tensor_tensor(ex, best, best[:, :, 0:1].to_broadcast([R, HEADS, TOPK]), ALU.subtract))
                    for h in range(HEADS):
                        last = dve.max_index(pos[:, h, :], best[:, h, :], comb[:, 64 * h:64 * (h + 1)])
                    link(last)
                    dve.tensor_scalar(posi, pos, 3, None, ALU.logical_shift_right)
                    link(dve.tensor_scalar(posj, pos, TOPK - 1, None, ALU.bitwise_and))
                    for pp, a, res in ((posi, 0, hi_f), (posj, 1, lo_f)):
                        link(dve.tensor_tensor(eq4, pp.unsqueeze(3).to_broadcast(H3),
                                               iota8[:, :].unsqueeze(1).unsqueeze(1).to_broadcast(H3), ALU.is_equal))
                        link(dve.tensor_tensor(eq4, eq4, topf[:, :, a, :].unsqueeze(2).to_broadcast(H3), ALU.mult))
                        link(dve.tensor_reduce(res, eq4, AX, ALU.add))
                    dve.scalar_tensor_tensor(idx[:, s, :], hi_f.rearrange("p h k -> p (h k)"), float(NKEYS),
                                             lo_f.rearrange("p h k -> p (h k)"), ALU.mult, ALU.add).then_inc(f_idx, 1)
                    dve.wait_ge(f_e, tq + 1)
                    link(dve.tensor_reduce(es, ex, AX, ALU.add))
                    dve.reciprocal(er, es).then_inc(f_rc, 1)
                    dve.wait_ge(f_rc, tq + 1)
                    dve.tensor_tensor(prob[:, s], ex, er.unsqueeze(2).to_broadcast([R, HEADS, TOPK]), ALU.mult)\
                       .then_inc(f_prob, 1)
                    assert n[0] == FIN

                NODE_PARTS = (node_sum, node_x, node_clamp, node_mish, node_y, None, node_x2, node_xf)

                def output(t, s):
                    dve.wait_ge(f_xr, t + 1)
                    dve.wait_ge(f_pe, (t + 1) * PICKS)
                    dve.tensor_tensor(xr[:, s, :], banks[s][0:R, :], xr[:, s, :], ALU.add).then_inc(f_o, 1)

                dve.wait_ge(c_wlate, 160)
                node_sum(0)
                node_rest(0)
                for h in range(HEADS):
                    look_up_head(0, h)
                    if h == 4:
                        node_sum(1)
                finish(0, 0)
                node_rest(1)

                def tile(s, i, look, node):
                    t = 2 * i + s
                    dve.wait_ge(f_xc, t + 1)
                    dve.wait_ge(f_prob, t + 1)
                    for h in range(HEADS):
                        for k in range(TOPK):
                            j = h * TOPK + k
                            dve.wait_ge(f_w[j % RING], 16 * (t * slot_uses(j % RING) + j // RING + 1))
                            need(dve, f_in, t * PICKS + j - 1)
                            dve.scalar_tensor_tensor(junk[:, j % 2, :], ring[j % RING][:, 0:D], 1.0, xc[:, s, :],
                                                     ALU.mult, ALU.mult, accum_out=inner[:, h % 2, k:k + 1])\
                               .then_inc(f_in, 1)
                        dve.wait_ge(f_in, t * PICKS + (h + 1) * TOPK)
                        if not static(t) or t * HEADS + h >= 2:
                            dve.wait_ge(f_dg, (t * HEADS + h - 1) * TOPK)
                        dve.scalar_tensor_tensor(vals[:, h % 2, :], inner[:, h % 2, :], 0.0, prob[:, s, h, :],
                                                 ALU.max, ALU.mult).then_inc(f_val, 1)
                        if look and 1 <= h <= 4:
                            look_up_head(t + 1, 2 * h - 2)
                            look_up_head(t + 1, 2 * h - 1)
                        if node and h != 5:
                            NODE_PARTS[h](t + 2)
                        if h == 1 and (not static(t) or t > 0):
                            output(t - 1, 1 - s)
                        if look and h == 5:
                            finish(t + 1, 1 - s)
                run_tiles(dve, tile)
                output(NT - 1, 1)

            @block.tensor
            def _(pe):
                def transposes(bank, rows):
                    for k in range(KC):
                        last = pe.transpose(bank[:, 128 * k:128 * k + R], rows[:, 128 * k:128 * (k + 1)],
                                            ident[0:R, 0:R])
                    return last

                def products(bank, cols, w, first=True, last=True):
                    for k in range(KC):
                        product = pe.matmul(bank[0:R, :], cols[:, k, 0:R], w[:, k, :],
                                            start=(first and k == 0), stop=(last and k == KC - 1))
                    return product

                def node_Tx(u):
                    pe.wait_ge(m_in2, 32 * (u + 1))
                    need(pe, m_y1, u)
                    transposes(banks[3], XN[:, 0, :]).then_inc(m_Tx, 1)

                def node_T(u):
                    pe.wait_ge(m_ag, u + 1)
                    need(pe, m_hT, u)
                    transposes(banks[2], A[:, 0, :]).then_inc(m_T, 1)

                def node_w3x(u):
                    pe.wait_ge(m_xT, u + 1)
                    products(banks[3], xnT3, w3x, last=False)

                def node_w3(u):
                    pe.wait_ge(m_aT, u + 1)
                    products(banks[3], aT, w3a, first=False).then_inc(m_3, 1)

                def node_T2(u):
                    pe.wait_ge(m_h, u + 1)
                    transposes(banks[2], MX).then_inc(m_T2, 1)

                def node_w4(u):
                    pe.wait_ge(m_hT, u + 1)
                    pe.wait_ge(m_x, u + 1)
                    products(banks[3], aT, w4).then_inc(m_4, 1)

                def node_all(u):
                    for part in (node_Tx, node_T, node_w3x, node_w3, node_T2, node_w4):
                        part(u)

                def transposed(tq):
                    pe.wait_ge(m_xf, tq + 1)
                    need(pe, f_qs, tq * HEADS)
                    transposes(banks[4], xfn).then_inc(f_T, 1)

                def queries(tq, h):
                    q = tq * HEADS + h
                    pe.wait_ge(f_xT, tq + 1)
                    need(pe, f_qs, q - 1)
                    for k in range(KC):
                        last = pe.matmul(q_bank[h % 2][:, 0:R], wq[:, k, 128 * h:128 * (h + 1)], xqT[:, k, 0:R],
                                         start=(k == 0), stop=(k == KC - 1))
                    last.then_inc(f_q, 1)

                def scores(tq, h):
                    q = tq * HEADS + h
                    pe.wait_ge(f_qs, q + 1)
                    need(pe, f_top, q - 1)
                    for a in range(2):
                        half = slice(HALF * a, HALF * (a + 1))
                        if a:
                            pe.wait_ge(f_s, 2 * q + 1)
                        pe.matmul(s_bank[h % 2][0:R, NKEYS * a:NKEYS * (a + 1)], qh[half, h % 2, 0:R],
                                         keys[half, NKEYS * h:NKEYS * (h + 1)], start=True, stop=True).then_inc(f_s, 1)

                def keep_clock(n):
                    for _ in range(n):
                        pe.matmul(banks[1][:, :], ident[:, :], w3x[:, 0, :], start=True, stop=True)

                pe.wait_ge(c_wlate, 160)
                keep_clock(4)
                node_all(0)
                keep_clock(8)
                transposed(0)
                queries(0, 0)
                for h in range(HEADS):
                    if h + 1 < HEADS:
                        queries(0, h + 1)
                    scores(0, h)
                node_all(1)
                keep_clock(8)

                def tile(s, i, look, node):
                    t = 2 * i + s
                    for h in range(1, HEADS + 1):
                        if look and h == 1:
                            transposed(t + 1)
                        if node and h == 1:
                            node_Tx(t + 2)
                            node_T(t + 2)
                        if node and h == 4:
                            node_T2(t + 2)
                        if look and h <= 4:
                            for part in (queries, scores):
                                part(t + 1, 2 * h - 2)
                                part(t + 1, 2 * h - 1)
                        if node and h == 1:
                            node_w3x(t + 2)
                            node_w3(t + 2)
                        if node and h == 4:
                            node_w4(t + 2)
                        for k in range(TOPK):
                            j = (h - 1) * TOPK + k
                            pe.wait_ge(f_dg, t * PICKS + j + 1)
                            if j == 0:
                                need(pe, f_o, t - 1)
                            pe.matmul(banks[s][0:R, :], dg[:, j % DSLOTS, 0:R], ring[j % RING][:, D:2 * D],
                                      start=(j == 0), stop=(j == PICKS - 1)).then_inc(f_pe, 1)
                run_tiles(pe, tile)


def kernel(**inputs):
    import numpy as np
    import concourse.bacc as bacc
    from concourse import mybir as mb
    from concourse.bass_utils import run_bass_kernel_spmd

    a = {k: np.asarray(v) for k, v in inputs.items()}
    rows = 125
    src, dst, ea = a["src"], a["dst"], a["edge_attr_64"]
    keys = a["L0_ffn_keys"]
    heads, halves, n_keys, width = keys.shape
    laid = {
        "x": a["x"],
        "src_cols": src.reshape(rows, -1),
        "dst_cols": dst.reshape(rows, -1),
        "dst_row": dst.reshape(rows, -1).T.reshape(1, -1),
        "ea_t": ea.reshape(rows, -1, ea.shape[1]).transpose(2, 1, 0).reshape(ea.shape[1], -1),
        **{n: a[f"L0_gnn_{n}"] for n in ("W1", "b1", "W2", "b2", "W3", "b3", "W4", "b4", "gamma", "beta")},
        "Wq": a["L0_ffn_Wq"],
        "bq_cols": a["L0_ffn_bq"].reshape(heads, -1).T,
        "keys_t": keys.transpose(1, 3, 0, 2).reshape(halves * width, heads * n_keys),
        "w_du": np.concatenate([a["L0_ffn_w_down"], a["L0_ffn_w_up"]], axis=1),
    }
    nc = bacc.Bacc("TRN2", target_bir_lowering=False, num_devices=1)
    arrays, args = {}, []
    for name, v in laid.items():
        v = np.ascontiguousarray(v)
        arrays[f"in_{name}"] = v
        args.append(nc.dram_tensor(f"in_{name}", v.shape, mb.dt.from_np(v.dtype), kind="ExternalInput").ap())
    out = nc.dram_tensor("out_0", a["x"].shape, mb.dt.float32, kind="ExternalOutput").ap()
    gnn_peer_kernel(nc, *args, out)
    r = run_bass_kernel_spmd(nc, [arrays], core_ids=[0])
    return r.results[0]["out_0"]
```
